# Optimizing a Trainium2 kernel written in Bass

```python
import numpy as np
import jax
import jax.numpy as jnp

def _softmax(x, axis=-1):
    return jax.nn.softmax(x, axis=axis)

def _gelu(x):
    return jax.nn.gelu(x, approximate=True)

def _silu(x):
    return jax.nn.silu(x)

def _sigmoid(x):
    return jax.nn.sigmoid(x)

def _layernorm(x, axis=-1, eps=1e-05):
    m = jnp.mean(x, axis=axis, keepdims=True)
    v = jnp.var(x, axis=axis, keepdims=True)
    return (x - m) / jnp.sqrt(v + eps)

def _scatter_add(tgt, idx, src, axis=0):
    return tgt.at[idx].add(src)

def _segment_sum(src, seg, n):
    return jax.ops.segment_sum(src, seg, n)
kernel_name = 'mk_seq_postln_d2_jaxref_r8_e4efaf'

def setup_inputs(seed: int=0):
    np.random.seed(seed)
    _w = jnp.asarray

    def _L0_attn_setup():
        import jax, jax.numpy as jnp
        import numpy as np

        def _rotate_every_two(x):
            x1 = x[..., ::2]
            x2 = x[..., 1::2]
            return jnp.stack((-x2, x1), axis=-1).reshape(x.shape)
        key = jax.random.key(seed)
        ks = jax.random.split(key, 6)
        B, S, D = (2, 256, 128)
        w = lambda k, shape: jax.random.normal(k, shape, dtype=jnp.float32) * 0.02
        return {'x': jax.random.normal(ks[0], (B, S, D), dtype=jnp.float32), 'Wq': w(ks[1], (D, D)), 'bq': jnp.zeros((D,), jnp.float32), 'Wk': w(ks[2], (D, D)), 'bk': jnp.zeros((D,), jnp.float32), 'Wv': w(ks[3], (D, 2 * D)), 'bv': jnp.zeros((2 * D,), jnp.float32), 'Wg': w(ks[4], (D, 2 * D)), 'bg': jnp.zeros((2 * D,), jnp.float32), 'Wo': w(ks[5], (2 * D, D)), 'bo': jnp.zeros((D,), jnp.float32)}
    _L0_attn_in = _L0_attn_setup()

    def _L0_ffn_setup():
        import jax, jax.numpy as jnp
        import numpy as np
        DIM = 128
        DEPTH = 2
        HEADS = 8
        DIM_HEAD = 64
        WINDOW = 64
        INNER = HEADS * DIM_HEAD
        HID = int(DIM * 4 * 2 / 3)
        B, N = (2, 1024)
        QK_SCALE = 8.0

        def shift_token(t):
            t1, t2 = jnp.split(t, 2, axis=-1)
            t2 = jnp.pad(t2, ((0, 0), (1, 0), (0, 0)))[:, :-1]
            return jnp.concatenate([t1, t2], axis=-1)

        def l2norm(t):
            return t / jnp.clip(jnp.linalg.norm(t, axis=-1, keepdims=True), 1e-12)

        def rotate_half(x):
            x1, x2 = jnp.split(x, 2, axis=-1)
            return jnp.concatenate([-x2, x1], axis=-1)

        def rotary_xpos(q, k):
            n = q.shape[-2]
            half_idx = jnp.arange(0, DIM_HEAD, 2, dtype=jnp.float32)
            inv_freq = 1.0 / 10000.0 ** (half_idx / DIM_HEAD)
            t = jnp.arange(n, dtype=jnp.float32)
            freqs = t[:, None] * inv_freq[None, :]
            freqs = jnp.concatenate([freqs, freqs], axis=-1)
            base = (half_idx + 0.4 * DIM_HEAD) / (1.4 * DIM_HEAD)
            power = (t - n // 2) / float(WINDOW // 2)
            scale = base[None, :] ** power[:, None]
            scale = jnp.concatenate([scale, scale], axis=-1)
            cos, sin = (jnp.cos(freqs), jnp.sin(freqs))
            q = q * cos * scale + rotate_half(q) * sin * scale
            k = k * cos / scale + rotate_half(k) * sin / scale
            return (q, k)

        def local_attention(q, k, v):
            b, h, n, d = q.shape
            w = n // WINDOW
            bq = q.reshape(b, h, w, WINDOW, d) * QK_SCALE
            bk = k.reshape(b, h, w, WINDOW, d)
            bv = v.reshape(b, h, w, WINDOW, d)

            def look_around(t):
                p = jnp.pad(t, ((0, 0), (0, 0), (1, 0), (0, 0), (0, 0)))
                return jnp.concatenate([p[:, :, :w], p[:, :, 1:]], axis=3)
            bk, bv = (look_around(bk), look_around(bv))
            bt = jnp.arange(n).reshape(w, WINDOW)
            btp = jnp.pad(bt, ((1, 0), (0, 0)), constant_values=-1)
            btk = jnp.concatenate([btp[:w], btp[1:]], axis=1)
            sim = jnp.einsum('bhwid,bhwjd->bhwij', bq, bk)
            i = bt[:, :, None]
            j = btk[:, None, :]
            mask = (i < j) | (i > j + WINDOW) | (j == -1)
            sim = jnp.where(mask, -jnp.finfo(sim.dtype).max, sim)
            attn = jax.nn.softmax(sim, axis=-1)
            out = jnp.einsum('bhwij,bhwjd->bhwid', attn, bv)
            return out.reshape(b, h, n, d)

        def _layer(x, wqkv, qs, ksc, wo, lg, lb, w1, b1, w2, b2):
            b, n, _ = x.shape
            h = shift_token(x)
            qkv = h @ wqkv
            q, k, v = jnp.split(qkv, 3, axis=-1)
            to_heads = lambda t: t.reshape(b, n, HEADS, DIM_HEAD).transpose(0, 2, 1, 3)
            q, k, v = (to_heads(q), to_heads(k), to_heads(v))
            q = l2norm(q) * qs
            k = l2norm(k) * ksc
            q, k = rotary_xpos(q, k)
            o = local_attention(q, k, v)
            o = o.transpose(0, 2, 1, 3).reshape(b, n, INNER)
            x = x + o @ wo
            h = shift_token(x)
            mu = h.mean(-1, keepdims=True)
            var = h.var(-1, keepdims=True)
            h = (h - mu) / jnp.sqrt(var + 1e-05) * lg + lb
            h = h @ w1 + b1
            a, g = jnp.split(h, 2, axis=-1)
            h = a * jax.nn.gelu(g, approximate=False)
            x = x + h @ w2 + b2
            return x
        key = jax.random.key(seed)
        ks = jax.random.split(key, 6)
        return {'x': jax.random.normal(ks[0], (B, N, DIM), jnp.float32), 'wqkv': jax.random.normal(ks[1], (DEPTH, DIM, 3 * INNER), jnp.float32) * 0.02, 'q_scale': jnp.ones((DEPTH, DIM_HEAD), jnp.float32), 'k_scale': jnp.ones((DEPTH, DIM_HEAD), jnp.float32), 'wo': jax.random.normal(ks[2], (DEPTH, INNER, DIM), jnp.float32) * 0.02, 'ln_g': jnp.ones((DEPTH, DIM), jnp.float32), 'ln_b': jnp.zeros((DEPTH, DIM), jnp.float32), 'w1': jax.random.normal(ks[3], (DEPTH, DIM, 2 * HID), jnp.float32) * 0.02, 'b1': jnp.zeros((DEPTH, 2 * HID), jnp.float32), 'w2': jax.random.normal(ks[4], (DEPTH, HID, DIM), jnp.float32) * 0.02, 'b2': jnp.zeros((DEPTH, DIM), jnp.float32)}
    _L0_ffn_in = _L0_ffn_setup()

    def _L1_attn_setup():
        import jax, jax.numpy as jnp
        import numpy as np
        EMB = 128
        HEADS = 16
        HEADSIZE = EMB // HEADS
        EPS = 1e-05

        def _layernorm(x, g, b):
            m = jnp.mean(x, axis=-1, keepdims=True)
            v = jnp.mean((x - m) ** 2, axis=-1, keepdims=True)
            return (x - m) * jax.lax.rsqrt(v + EPS) * g + b
        key = jax.random.key(seed)
        ks = jax.random.split(key, 6)
        B, T = (4, 256)
        s = 1.0 / np.sqrt(EMB)
        return {'x': jax.random.normal(ks[0], (B, T, EMB), dtype=jnp.float32), 'Wk': jax.random.normal(ks[1], (EMB, EMB), dtype=jnp.float32) * s, 'Wq': jax.random.normal(ks[2], (EMB, EMB), dtype=jnp.float32) * s, 'Wv': jax.random.normal(ks[3], (EMB, EMB), dtype=jnp.float32) * s, 'Wo': jax.random.normal(ks[4], (EMB, EMB), dtype=jnp.float32) * s, 'bo': jnp.zeros((EMB,), dtype=jnp.float32), 'kln_g': jnp.ones((HEADSIZE,), dtype=jnp.float32), 'kln_b': jnp.zeros((HEADSIZE,), dtype=jnp.float32), 'qln_g': jnp.ones((HEADSIZE,), dtype=jnp.float32), 'qln_b': jnp.zeros((HEADSIZE,), dtype=jnp.float32)}
    _L1_attn_in = _L1_attn_setup()

    def _L1_ffn_setup():
        import jax, jax.numpy as jnp
        import numpy as np
        D_IN, D_HID = (128, 512)

        def _ternary(key, shape):
            return jax.random.randint(key, shape, -1, 2).astype(jnp.float32)

        def _tlin(x, w, s):
            return jnp.einsum('bsi,oi->bso', x, w) * s
        key = jax.random.key(seed)
        ks = jax.random.split(key, 12)
        inv = lambda fan: 1.0 / np.sqrt(fan).astype(np.float32)
        return {'x': jax.random.normal(ks[0], (4, 256, D_IN), dtype=jnp.float32), 'w1_w': _ternary(ks[1], (D_HID, D_IN)), 'w1_s': jax.random.uniform(ks[2], (D_HID,), dtype=jnp.float32) * inv(D_IN), 'w2_w': _ternary(ks[3], (D_HID, D_IN)), 'w2_s': jax.random.uniform(ks[4], (D_HID,), dtype=jnp.float32) * inv(D_IN), 'h1_w': _ternary(ks[5], (D_HID, D_HID)), 'h1_s': jax.random.uniform(ks[6], (D_HID,), dtype=jnp.float32) * inv(D_HID), 'h2_w': _ternary(ks[7], (D_HID, D_HID)), 'h2_s': jax.random.uniform(ks[8], (D_HID,), dtype=jnp.float32) * inv(D_HID), 'w3_w': _ternary(ks[9], (D_IN, D_HID)), 'w3_s': jax.random.uniform(ks[10], (D_IN,), dtype=jnp.float32) * inv(D_HID)}
    _L1_ffn_in = _L1_ffn_setup()
    _d = {'L0_attn_x': _L0_attn_in['x'], 'L0_attn_Wq': _L0_attn_in['Wq'], 'L0_attn_bq': _L0_attn_in['bq'], 'L0_attn_Wk': _L0_attn_in['Wk'], 'L0_attn_bk': _L0_attn_in['bk'], 'L0_attn_Wv': _L0_attn_in['Wv'], 'L0_attn_bv': _L0_attn_in['bv'], 'L0_attn_Wg': _L0_attn_in['Wg'], 'L0_attn_bg': _L0_attn_in['bg'], 'L0_attn_Wo': _L0_attn_in['Wo'], 'L0_attn_bo': _L0_attn_in['bo'], 'L0_ffn_wqkv': _L0_ffn_in['wqkv'], 'L0_ffn_q_scale': _L0_ffn_in['q_scale'], 'L0_ffn_k_scale': _L0_ffn_in['k_scale'], 'L0_ffn_wo': _L0_ffn_in['wo'], 'L0_ffn_ln_g': _L0_ffn_in['ln_g'], 'L0_ffn_ln_b': _L0_ffn_in['ln_b'], 'L0_ffn_w1': _L0_ffn_in['w1'], 'L0_ffn_b1': _L0_ffn_in['b1'], 'L0_ffn_w2': _L0_ffn_in['w2'], 'L0_ffn_b2': _L0_ffn_in['b2'], 'L1_attn_Wk': _L1_attn_in['Wk'], 'L1_attn_Wq': _L1_attn_in['Wq'], 'L1_attn_Wv': _L1_attn_in['Wv'], 'L1_attn_Wo': _L1_attn_in['Wo'], 'L1_attn_bo': _L1_attn_in['bo'], 'L1_attn_kln_g': _L1_attn_in['kln_g'], 'L1_attn_kln_b': _L1_attn_in['kln_b'], 'L1_attn_qln_g': _L1_attn_in['qln_g'], 'L1_attn_qln_b': _L1_attn_in['qln_b'], 'L1_ffn_w1_w': _L1_ffn_in['w1_w'], 'L1_ffn_w1_s': _L1_ffn_in['w1_s'], 'L1_ffn_w2_w': _L1_ffn_in['w2_w'], 'L1_ffn_w2_s': _L1_ffn_in['w2_s'], 'L1_ffn_h1_w': _L1_ffn_in['h1_w'], 'L1_ffn_h1_s': _L1_ffn_in['h1_s'], 'L1_ffn_h2_w': _L1_ffn_in['h2_w'], 'L1_ffn_h2_s': _L1_ffn_in['h2_s'], 'L1_ffn_w3_w': _L1_ffn_in['w3_w'], 'L1_ffn_w3_s': _L1_ffn_in['w3_s']}
    _x0 = _d['L0_attn_x']
    _d['L0_attn_x'] = jax.random.normal(jax.random.fold_in(jax.random.key(seed), 1), (4, 512, 128), dtype=_x0.dtype)
    del _x0
    return _d

def reference(L0_attn_x, L0_attn_Wq, L0_attn_bq, L0_attn_Wk, L0_attn_bk, L0_attn_Wv, L0_attn_bv, L0_attn_Wg, L0_attn_bg, L0_attn_Wo, L0_attn_bo, L0_ffn_wqkv, L0_ffn_q_scale, L0_ffn_k_scale, L0_ffn_wo, L0_ffn_ln_g, L0_ffn_ln_b, L0_ffn_w1, L0_ffn_b1, L0_ffn_w2, L0_ffn_b2, L1_attn_Wk, L1_attn_Wq, L1_attn_Wv, L1_attn_Wo, L1_attn_bo, L1_attn_kln_g, L1_attn_kln_b, L1_attn_qln_g, L1_attn_qln_b, L1_ffn_w1_w, L1_ffn_w1_s, L1_ffn_w2_w, L1_ffn_w2_s, L1_ffn_h1_w, L1_ffn_h1_s, L1_ffn_h2_w, L1_ffn_h2_s, L1_ffn_w3_w, L1_ffn_w3_s):

    def _L0_attn_ref(x, Wq, bq, Wk, bk, Wv, bv, Wg, bg, Wo, bo):
        import jax, jax.numpy as jnp
        import numpy as np

        def _rotate_every_two(x):
            x1 = x[..., ::2]
            x2 = x[..., 1::2]
            return jnp.stack((-x2, x1), axis=-1).reshape(x.shape)
        B, S, D = x.shape
        H = 16
        key_dim = D // H
        head_dim = 2 * D // H
        scaling = key_dim ** (-0.5)
        angle = 1.0 / 10000.0 ** jnp.linspace(0.0, 1.0, key_dim // 2)
        angle = jnp.repeat(angle, 2).astype(jnp.float32)
        decay = jnp.log(1.0 - 2.0 ** (-5.0 - jnp.arange(H, dtype=jnp.float32)))
        idx = jnp.arange(S, dtype=jnp.float32)
        sin = jnp.sin(idx[:, None] * angle[None, :])
        cos = jnp.cos(idx[:, None] * angle[None, :])
        diff = idx[:, None] - idx[None, :]
        mask = jnp.where(diff >= 0, jnp.exp(decay[:, None, None] * diff), 0.0)
        mask = mask / jnp.sqrt(mask.sum(-1, keepdims=True))
        q = (x @ Wq + bq).reshape(B, S, H, key_dim).transpose(0, 2, 1, 3)
        k = ((x @ Wk + bk) * scaling).reshape(B, S, H, key_dim).transpose(0, 2, 1, 3)
        v = x @ Wv + bv
        g = x @ Wg + bg
        qr = q * cos + _rotate_every_two(q) * sin
        kr = k * cos + _rotate_every_two(k) * sin
        vr = v.reshape(B, S, H, head_dim).transpose(0, 2, 1, 3)
        qk = jnp.einsum('bhsd,bhtd->bhst', qr, kr) * mask
        denom = jnp.clip(jnp.abs(jax.lax.stop_gradient(qk).sum(-1, keepdims=True)), 1.0, None)
        qk = qk / denom
        out = jnp.einsum('bhst,bhtd->bhsd', qk, vr).transpose(0, 2, 1, 3)
        mu = out.mean(-1, keepdims=True)
        var = ((out - mu) ** 2).mean(-1, keepdims=True)
        out = (out - mu) / jnp.sqrt(var + 1e-05)
        out = out.reshape(B, S, H * head_dim)
        out = jax.nn.silu(g) * out
        return out @ Wo + bo

    def _L0_ffn_ref(x, wqkv, q_scale, k_scale, wo, ln_g, ln_b, w1, b1, w2, b2):
        import jax, jax.numpy as jnp
        import numpy as np
        DIM = 128
        DEPTH = 2
        HEADS = 8
        DIM_HEAD = 64
        WINDOW = 64
        INNER = HEADS * DIM_HEAD
        HID = int(DIM * 4 * 2 / 3)
        B, N = (2, 1024)
        QK_SCALE = 8.0

        def shift_token(t):
            t1, t2 = jnp.split(t, 2, axis=-1)
            t2 = jnp.pad(t2, ((0, 0), (1, 0), (0, 0)))[:, :-1]
            return jnp.concatenate([t1, t2], axis=-1)

        def l2norm(t):
            return t / jnp.clip(jnp.linalg.norm(t, axis=-1, keepdims=True), 1e-12)

        def rotate_half(x):
            x1, x2 = jnp.split(x, 2, axis=-1)
            return jnp.concatenate([-x2, x1], axis=-1)

        def rotary_xpos(q, k):
            n = q.shape[-2]
            half_idx = jnp.arange(0, DIM_HEAD, 2, dtype=jnp.float32)
            inv_freq = 1.0 / 10000.0 ** (half_idx / DIM_HEAD)
            t = jnp.arange(n, dtype=jnp.float32)
            freqs = t[:, None] * inv_freq[None, :]
            freqs = jnp.concatenate([freqs, freqs], axis=-1)
            base = (half_idx + 0.4 * DIM_HEAD) / (1.4 * DIM_HEAD)
            power = (t - n // 2) / float(WINDOW // 2)
            scale = base[None, :] ** power[:, None]
            scale = jnp.concatenate([scale, scale], axis=-1)
            cos, sin = (jnp.cos(freqs), jnp.sin(freqs))
            q = q * cos * scale + rotate_half(q) * sin * scale
            k = k * cos / scale + rotate_half(k) * sin / scale
            return (q, k)

        def local_attention(q, k, v):
            b, h, n, d = q.shape
            w = n // WINDOW
            bq = q.reshape(b, h, w, WINDOW, d) * QK_SCALE
            bk = k.reshape(b, h, w, WINDOW, d)
            bv = v.reshape(b, h, w, WINDOW, d)

            def look_around(t):
                p = jnp.pad(t, ((0, 0), (0, 0), (1, 0), (0, 0), (0, 0)))
                return jnp.concatenate([p[:, :, :w], p[:, :, 1:]], axis=3)
            bk, bv = (look_around(bk), look_around(bv))
            bt = jnp.arange(n).reshape(w, WINDOW)
            btp = jnp.pad(bt, ((1, 0), (0, 0)), constant_values=-1)
            btk = jnp.concatenate([btp[:w], btp[1:]], axis=1)
            sim = jnp.einsum('bhwid,bhwjd->bhwij', bq, bk)
            i = bt[:, :, None]
            j = btk[:, None, :]
            mask = (i < j) | (i > j + WINDOW) | (j == -1)
            sim = jnp.where(mask, -jnp.finfo(sim.dtype).max, sim)
            attn = jax.nn.softmax(sim, axis=-1)
            out = jnp.einsum('bhwij,bhwjd->bhwid', attn, bv)
            return out.reshape(b, h, n, d)

        def _layer(x, wqkv, qs, ksc, wo, lg, lb, w1, b1, w2, b2):
            b, n, _ = x.shape
            h = shift_token(x)
            qkv = h @ wqkv
            q, k, v = jnp.split(qkv, 3, axis=-1)
            to_heads = lambda t: t.reshape(b, n, HEADS, DIM_HEAD).transpose(0, 2, 1, 3)
            q, k, v = (to_heads(q), to_heads(k), to_heads(v))
            q = l2norm(q) * qs
            k = l2norm(k) * ksc
            q, k = rotary_xpos(q, k)
            o = local_attention(q, k, v)
            o = o.transpose(0, 2, 1, 3).reshape(b, n, INNER)
            x = x + o @ wo
            h = shift_token(x)
            mu = h.mean(-1, keepdims=True)
            var = h.var(-1, keepdims=True)
            h = (h - mu) / jnp.sqrt(var + 1e-05) * lg + lb
            h = h @ w1 + b1
            a, g = jnp.split(h, 2, axis=-1)
            h = a * jax.nn.gelu(g, approximate=False)
            x = x + h @ w2 + b2
            return x
        for l in range(DEPTH):
            x = _layer(x, wqkv[l], q_scale[l], k_scale[l], wo[l], ln_g[l], ln_b[l], w1[l], b1[l], w2[l], b2[l])
        return x

    def _L1_attn_ref(x, Wk, Wq, Wv, Wo, bo, kln_g, kln_b, qln_g, qln_b):
        import jax, jax.numpy as jnp
        import numpy as np
        EMB = 128
        HEADS = 16
        HEADSIZE = EMB // HEADS
        EPS = 1e-05

        def _layernorm(x, g, b):
            m = jnp.mean(x, axis=-1, keepdims=True)
            v = jnp.mean((x - m) ** 2, axis=-1, keepdims=True)
            return (x - m) * jax.lax.rsqrt(v + EPS) * g + b
        B, T, E = x.shape
        k = jnp.einsum('bte,fe->btf', x, Wk).reshape(B, T, HEADS, HEADSIZE)
        q = jnp.einsum('bte,fe->btf', x, Wq).reshape(B, T, HEADS, HEADSIZE)
        v = jnp.einsum('bte,fe->btf', x, Wv).reshape(B, T, HEADS, HEADSIZE)
        k = _layernorm(k, kln_g, kln_b)
        q = _layernorm(q, qln_g, qln_b)
        scale = E ** (-0.25)
        q = q * scale
        k = k * scale
        dot = jnp.einsum('bihd,bjhd->bhij', q, k)
        causal = jnp.triu(jnp.ones((T, T), dtype=bool), k=1)
        dot = jnp.where(causal, -jnp.inf, dot)
        att = jax.nn.softmax(dot, axis=-1)
        out = jnp.einsum('bhij,bjhd->bihd', att, v).reshape(B, T, E)
        return jnp.einsum('bte,fe->btf', out, Wo) + bo

    def _L1_ffn_ref(x, w1_w, w1_s, w2_w, w2_s, h1_w, h1_s, h2_w, h2_s, w3_w, w3_s):
        import jax, jax.numpy as jnp
        import numpy as np
        D_IN, D_HID = (128, 512)

        def _ternary(key, shape):
            return jax.random.randint(key, shape, -1, 2).astype(jnp.float32)

        def _tlin(x, w, s):
            return jnp.einsum('bsi,oi->bso', x, w) * s
        h = jax.nn.silu(_tlin(x, w1_w, w1_s)) * _tlin(x, w2_w, w2_s)
        h = jax.nn.gelu(_tlin(h, h1_w, h1_s), approximate=False)
        h = jax.nn.gelu(_tlin(h, h2_w, h2_s), approximate=False)
        return _tlin(h, w3_w, w3_s)
    x = L0_attn_x
    x = _layernorm(x + _L0_attn_ref(x, L0_attn_Wq, L0_attn_bq, L0_attn_Wk, L0_attn_bk, L0_attn_Wv, L0_attn_bv, L0_attn_Wg, L0_attn_bg, L0_attn_Wo, L0_attn_bo), axis=-1)
    x = _layernorm(x + _L0_ffn_ref(x, L0_ffn_wqkv, L0_ffn_q_scale, L0_ffn_k_scale, L0_ffn_wo, L0_ffn_ln_g, L0_ffn_ln_b, L0_ffn_w1, L0_ffn_b1, L0_ffn_w2, L0_ffn_b2), axis=-1)
    x = _layernorm(x + _L1_attn_ref(x, L1_attn_Wk, L1_attn_Wq, L1_attn_Wv, L1_attn_Wo, L1_attn_bo, L1_attn_kln_g, L1_attn_kln_b, L1_attn_qln_g, L1_attn_qln_b), axis=-1)
    x = _layernorm(x + _L1_ffn_ref(x, L1_ffn_w1_w, L1_ffn_w1_s, L1_ffn_w2_w, L1_ffn_w2_s, L1_ffn_h1_w, L1_ffn_h1_s, L1_ffn_h2_w, L1_ffn_h2_s, L1_ffn_w3_w, L1_ffn_w3_s), axis=-1)
    return x

_drawn_inputs = setup_inputs


def setup_inputs(seed=0):
    import zlib

    import numpy as np

    out = dict(_drawn_inputs(seed))
    spreads = {'L0_attn_bq': (0.0, 0.448),
     'L0_attn_bk': (0.0, 0.287),
     'L0_attn_bv': (0.0, 0.289),
     'L0_attn_bg': (0.0, 0.5),
     'L0_attn_bo': (0.0, 0.1),
     'L0_ffn_q_scale': (1.0, 0.6),
     'L0_ffn_k_scale': (1.0, 0.6),
     'L0_ffn_ln_g': (1.0, 0.6),
     'L0_ffn_ln_b': (0.0, 0.8),
     'L0_ffn_b1': (0.0, 0.8),
     'L0_ffn_b2': (0.0, 0.277),
     'L1_attn_bo': (0.0, 0.1),
     'L1_attn_kln_g': (1.0, 0.6),
     'L1_attn_kln_b': (0.0, 2.0),
     'L1_attn_qln_g': (1.0, 0.6),
     'L1_attn_qln_b': (0.0, 0.8)}
    factors = {'L0_ffn_wqkv': 3.054,
     'L0_ffn_wo': 2.98,
     'L0_ffn_w1': 6.237,
     'L0_ffn_w2': 6.099,
     'L1_ffn_w1_w': 8.0,
     'L1_ffn_w1_s': 8.0,
     'L1_ffn_w2_w': 8.0,
     'L1_ffn_w2_s': 8.0,
     'L1_ffn_h1_w': 8.0,
     'L1_ffn_h1_s': 8.0,
     'L1_ffn_h2_w': 8.0,
     'L1_ffn_h2_s': 8.0,
     'L1_ffn_w3_w': 8.0,
     'L1_ffn_w3_s': 8.0}
    for name, (base, spread) in spreads.items():
        noise = np.random.default_rng([zlib.crc32(name.encode()), seed]).standard_normal(out[name].shape)
        drawn = base * np.exp(spread * noise) if base else spread * noise
        out[name] = jnp.asarray(drawn.astype(out[name].dtype))
    for name, factor in factors.items():
        out[name] = (out[name] * factor).astype(out[name].dtype)
    return out
```

```python
from contextlib import ExitStack

import concourse.bass as bass
from concourse import mybir

ALU = mybir.AluOpType
ACT = mybir.ActivationFunctionType
F32 = mybir.dt.float32
F32R = mybir.dt.float32r
BF16 = mybir.dt.bfloat16
AX = mybir.AxisListType.X

P = 128
S = 512
NT = 4
G = 8
D = 128
H1, K1, V1 = 16, 8, 16
H2, D2, WIN = 8, 64, 64
HID = 341
KB = [128, 128, 85]
H3, D3 = 16, 8
EPS = 1e-5


def offsets(parts):
    at, out = 0, {}
    for name, width in parts:
        out[name] = (at, width)
        at += width
    return out, at


WEIGHTS, WEIGHTS_WIDTH = offsets(
    [("qk1", 4 * D), ("vg1", 512), ("wo1", 2 * D), ("bqk1", 4)]
    + [(f"{n}{l}", w) for l in range(2) for n, w in
       (("qkv2_", 1536), ("wo2_", 4 * D), ("w1_", 2 * HID), ("w2_", 3 * D), ("b1_", 6), ("ln2_", 2))]
    + [("qkv3", 3 * D), ("wo3", D)]
    + [("f1", 512), ("f2", 512), ("h1", 2048), ("h2", 2048), ("w3", 4 * D), ("s4", 16)])
WEIGHT_CUTS = [0, WEIGHTS["qkv2_0"][0], WEIGHTS["qkv2_1"][0], WEIGHTS["f1"][0], WEIGHTS_WIDTH]
ROWS, ROWS_WIDTH = offsets(
    [("bvg1", 512), ("bo1", D), ("b2_0", D), ("b2_1", D), ("bo3", D), ("s3", D),
     ("g3", 256), ("b3", 256), ("qs0", 256), ("qs1", 256)])
CONSTS, CONSTS_WIDTH = offsets(
    [("ident", 128), ("rot1", 4 * S), ("headmask", H1), ("statemask", H1 * (V1 + 1)), ("chunkdecay", 1),
     ("causal1", 128), ("rot2", NT * 4 * D2), ("band_first", 128), ("band", 128),
     ("mask_ij", 128), ("mask_ji", 128), ("shift", 128), ("carry", 128)])


def build(nc, x, wts, rows, consts, out):
    with ExitStack() as ctx:
        def sb(name, shape, dt=F32):
            return ctx.enter_context(nc.sbuf_tensor(name, shape, dt))

        def sem(name):
            return ctx.enter_context(nc.semaphore(name))

        W = sb("weights", [P, WEIGHTS_WIDTH])
        R = sb("rowconsts", [P, ROWS_WIDTH])
        C = sb("consts_sb", [P, CONSTS_WIDTH])
        xM = sb("x_tokens", [P, G, D])
        xi = sb("x_inner", [P, G, D])
        hT = sb("x_features", [P, 2, S + 1])
        table2 = sb("rotary2", [P, 2, 2, NT, 2, D2])
        mask_ij = sb("mask_ij_bf", [P, P], BF16)
        mask_ji = sb("mask_ji_bf", [P, P], BF16)
        ident_bf = sb("ident_bf", [P, P], BF16)
        neghalf = sb("neghalf", [P, 1])
        stats = sb("bn", [P, 12])
        meanvar = sb("meanvar", [P, 4, 2])
        vareps = sb("vareps", [P, 4])
        rstd = sb("rstd", [P, 4])
        qS = sb("q_strips", [P, 2, S], F32R)
        qS2 = sb("q_strips_shifted", [P, 2, S], F32R)
        kx = sb("k_strips", [P, 2, 4, S], F32R)
        hi3 = sb("hi3", [P, 256], F32R)
        neg3 = sb("negmax3", [P, 16], F32R)
        ARENA = 19900
        arena = sb("arena", [P, ARENA])

        def carve(sizes):
            offs, end = offsets(sizes)
            assert end <= ARENA, end
            return {k: arena[:, a:a + w] for k, (a, w) in offs.items()}

        def w_(name):
            a, n = WEIGHTS[name]
            return W[:, a:a + n]

        def r_(name):
            a, n = ROWS[name]
            return R[:, a:a + n]

        def c_(name):
            a, n = CONSTS[name]
            return C[:, a:a + n]

        ident = c_("ident")
        VW = H1 * (V1 + 1)
        a1 = carve([("qT", 2 * S), ("kT", 2 * S), ("scaled", 4 * S), ("v", G * VW), ("gate", G * 256),
                    ("kM", 2 * S), ("state", 2 * VW), ("statetmp", VW), ("on", 256), ("cen", 512), ("sq", 256),
                    ("cg", 512), ("y", 512), ("yT", 512), ("z", 256), ("den", 16), ("mu", 16), ("gvar", 32),
                    ("grstd", 32), ("qx", 2048), ("PT", 2 * 2048)])
        qT1 = a1["qT"].rearrange("p (b s) -> p b s", b=2)
        kT1 = a1["kT"].rearrange("p (b s) -> p b s", b=2)
        scaled1 = a1["scaled"].rearrange("p (k s) -> p k s", k=4)
        v1 = a1["v"].rearrange("p (g h d) -> p g h d", g=G, h=H1)
        gate1 = a1["gate"].rearrange("p (g d) -> p g d", g=G)
        kM1 = a1["kM"].rearrange("p (g d) -> p g d", g=G)
        state = a1["state"].rearrange("p (b d) -> p b d", b=2)
        cen1 = a1["cen"].rearrange("p (i h d) -> p i h d", i=2, h=H1)
        on1 = a1["on"].rearrange("p (h d) -> p h d", h=H1)
        sq1 = a1["sq"].rearrange("p (h d) -> p h d", h=H1)
        cg1 = a1["cg"].rearrange("p (i h d) -> p i h d", i=2, h=H1)
        y1 = a1["y"].rearrange("p (i d) -> p i d", i=2)
        yT1 = a1["yT"].rearrange("p (i d) -> p i d", i=2)
        z1 = a1["z"].rearrange("p (i d) -> p i d", i=2)
        gvar1 = a1["gvar"].rearrange("p (i d) -> p i d", i=2)
        grstd1 = a1["grstd"].rearrange("p (i d) -> p i d", i=2)
        qx1 = a1["qx"].rearrange("p (h d) -> p h d", h=H1)
        PT1 = a1["PT"].rearrange("p (i h d) -> p i h d", i=2, h=H1)

        VA = H2 * (D2 + 1)
        a2 = carve([("kz", 2 * H2 * 192), ("sq", 1024), ("qk", 4096), ("qT", 2 * S), ("sm", 2 * 1024),
                    ("PT", 2 * 1024), ("vA", 4 * VA), ("vS", 4 * VA), ("o", 1024), ("oT", 1024), ("hn", 256),
                    ("ss", 32), ("rn", 32), ("mx", 8), ("rs", 8)])
        kz = a2["kz"].rearrange("p (i h j) -> p i h j", i=2, h=H2)
        sq2 = a2["sq"]
        qk2 = a2["qk"][:, 0:2048].rearrange("p (i d) -> p i d", i=2)
        straight2 = a2["qk"][:, 2048:3072]
        swapped2 = a2["qk"][:, 3072:4096]
        gel2 = a2["qk"][:, 0:1024].rearrange("p (i d) -> p i d", i=2)
        hh2 = a2["qk"][:, 1024:4096].rearrange("p (b k s) -> p b k s", b=2, k=3)
        qT2 = a2["qT"].rearrange("p (i m d) -> p i m d", i=2, m=4)
        sm2 = a2["sm"].rearrange("p (i h j) -> p i h j", i=2, h=H2)
        PT2 = a2["PT"].rearrange("p (i h j) -> p i h j", i=2, h=H2)
        vA2 = a2["vA"].rearrange("p (i h d) -> p i h d", i=4, h=H2)
        vS2 = a2["vS"].rearrange("p (i h d) -> p i h d", i=4, h=H2)
        o2 = a2["o"].rearrange("p (i h d) -> p i h d", i=2, h=H2)
        oT2 = a2["oT"].rearrange("p (i m d) -> p i m d", i=2, m=4)
        hn2 = a2["hn"].rearrange("p (i d) -> p i d", i=2)
        ss2 = a2["ss"].rearrange("p (i d) -> p i d", i=2)
        rn2 = a2["rn"].rearrange("p (i d) -> p i d", i=2)

        NSLOT = 8
        a3 = carve([("PT", NSLOT * S), ("QS", G * S), ("KS", G * S), ("vp", G * S), ("oS", 512), ("oN", G * D),
                    ("cen", 512), ("n", 256), ("sq", 256), ("z", 256), ("mu", 32), ("var", 64), ("rs", 64),
                    ("mx", 32), ("r", 16)])
        PT3 = a3["PT"].rearrange("p (i d) -> p i d", i=NSLOT)
        QS = a3["QS"].rearrange("p (g h r) -> p g h r", g=G, h=H3)
        KS = a3["KS"].rearrange("p (g h r) -> p g h r", g=G, h=H3)
        vp = a3["vp"].rearrange("p (g h r) -> p g h r", g=G, h=H3)
        oS3 = a3["oS"]
        oN3 = a3["oN"].rearrange("p (g h d) -> p g h d", g=G, h=H3)
        cen3 = a3["cen"].rearrange("p (i h d) -> p i h d", i=2, h=32)
        n3 = a3["n"].rearrange("p (h d) -> p h d", h=32)
        sq3 = a3["sq"].rearrange("p (h d) -> p h d", h=32)
        z3 = a3["z"].rearrange("p (i d) -> p i d", i=2)
        var3 = a3["var"].rearrange("p (i d) -> p i d", i=2)
        rs3 = a3["rs"].rearrange("p (i d) -> p i d", i=2)
        mx3 = a3["mx"].rearrange("p (i t h) -> p i t h", i=2, t=NT)
        r3 = a3["r"].rearrange("p (t h) -> p t h", t=NT)

        a4 = carve([("h0", 2 * 4 * S), ("h1", 2 * 4 * S), ("silu", 1024), ("z", 256), ("t", 256)])
        h04 = a4["h0"].rearrange("p (b k s) -> p b k s", b=2, k=4)
        h14 = a4["h1"].rearrange("p (b k s) -> p b k s", b=2, k=4)
        silu4 = a4["silu"].rearrange("p (i s) -> p i s", i=2)
        z4 = a4["z"].rearrange("p (i d) -> p i d", i=2)
        t4 = a4["t"].rearrange("p (i d) -> p i d", i=2)

        psum = [ctx.enter_context(nc.psum_tensor(f"bank{i}", [P, 512], F32)) for i in range(8)]

        loaded = [sem(f"weights_loaded{i}") for i in range(4)]
        consts_loaded = sem("consts_loaded")
        tables_ready = sem("tables_ready")
        arrived = sem("arrived")
        go = sem("go")
        settle = sem("settle")
        cleared = []

        def counter(name):
            s = sem(name)
            cleared.append(s)
            return s

        phase_done = counter("phase_done")
        x_loaded = [counter(f"x_loaded{b}") for b in range(2)]
        stored = counter("stored")
        dve_step = counter("dve_step")
        pool_step = counter("pool_step")
        pe_xT, xT_ready = counter("pe_xT"), counter("xT_ready")
        var_ready, rstd_ready = counter("var_ready"), counter("rstd_ready")
        xM_ready = counter("xM_ready")
        (pe_qk1, qk1_scaled, qkT_ready, pe_vg, gate_pre, gate_ready, pe_kM, kM_ready, ones_ready, xb1_ready,
         qx_ready, pe_sc, PT1_ready, pe_o1, pe_kv, state_ready, on_ready, cen_ready, gvar_ready, grstd_ready,
         cg_ready, y_ready, pe_yT, yT_ready, pe_wo1, z1_ready) = (counter(n) for n in (
             "pe_qk1", "qk1_scaled", "qkT_ready", "pe_vg", "gate_pre", "gate_ready", "pe_kM", "kM_ready",
             "ones_ready", "xb1_ready", "qx_ready", "pe_sc", "PT1_ready", "pe_o1", "pe_kv", "state_ready",
             "on_ready", "cen_ready", "gvar_ready", "grstd_ready", "cg_ready", "y_ready", "pe_yT", "yT_ready",
             "pe_wo1", "z1_ready"))
        (pads_ready, pe_hT, hT_ready, pe_q, pe_k, pe_v, sq_ready, ss_ready, rn_ready, qn_ready, swapped_ready,
         rot_ready, pe_qT, pe_kT, qT_ready, kz_ready, vA_ready, pe_S, sm_ready, smx_ready, P_ready, pe_PT,
         PT2_ready, pe_O, o_ready, pe_oT, oT_ready, pe_wo2, xa_ready, pe_hs, hn_ready, pe_wg, pe_wa, gel_ready,
         hh_ready, xb2_ready, pe_w2, xf_ready) = (counter(n) for n in (
             "pads_ready", "pe_hT", "hT_ready", "pe_q", "pe_k", "pe_v", "sq_ready", "ss_ready", "rn_ready",
             "qn_ready", "swapped_ready", "rot_ready", "pe_qT", "pe_kT", "qT_ready", "kz_ready", "vA_ready",
             "pe_S", "sm_ready", "smx_ready", "P_ready", "pe_PT", "PT2_ready", "pe_O", "o_ready", "pe_oT",
             "oT_ready", "pe_wo2", "xa_ready", "pe_hs", "hn_ready", "pe_wg", "pe_wa", "gel_ready", "hh_ready",
             "xb2_ready", "pe_w2", "xf_ready"))
        vS_landed = [counter(f"vS_landed{i}") for i in range(4)]
        (strips_blank, pe_qkv3, cen3_ready, v3_ready, var3_ready, rs3_ready, strips_ready, pe_qS, pe_kS, qS_ready,
         kxa_ready, kxd_ready, pe_A, mx_ready, negmax_ready, pe_qS2, qS2_ready, pe_B, E_ready, pe_V, oS_ready,
         pe_oS, oN_ready, pe_oN, oNT_ready, pe_wo3, z3_ready) = (counter(n) for n in (
             "strips_blank", "pe_qkv3", "cen3_ready", "v3_ready", "var3_ready", "rs3_ready", "strips_ready",
             "pe_qS", "pe_kS", "qS_ready", "kxa_ready", "kxd_ready", "pe_A", "mx_ready", "negmax_ready",
             "pe_qS2", "qS2_ready", "pe_B", "E_ready", "pe_V", "oS_ready", "pe_oS", "oN_ready", "pe_oN",
             "oNT_ready", "pe_wo3", "z3_ready"))
        xb3_ready = counter("xb3_ready")
        (pe_f1, pe_f2, silu_ready, h0_ready, pe_h1, h1_ready, pe_h2, h2_ready, pe_w3, z4_scaled, out_ready) = (
            counter(n) for n in ("pe_f1", "pe_f2", "silu_ready", "h0_ready", "pe_h1", "h1_ready", "pe_h2",
                                 "h2_ready", "pe_w3", "z4_scaled", "out_ready"))

        place = {}
        last = [None] * 8
        turn = [0]

        def take(pe, key, until, bank=None):
            if bank is None:
                bank = turn[0] % 7
                turn[0] += 1
            for s, v in last[bank] or []:
                pe.wait_ge(s, v)
            last[bank] = until
            place[key] = bank
            return psum[bank]

        def held(key):
            return psum[place[key]]

        def hn_seen(n):
            l, g = divmod(n, G)
            return (2 + G) * l + 2 + g + 1

        def phase_end(eng, k):
            eng.drain().then_inc(phase_done, 1)
            eng.wait_ge(phase_done, 4 * k)

        def pair_end(eng, it):
            eng.drain().then_inc(arrived, 1)
            eng.wait_ge(go, it + 1)
            eng.sem_inc(settle)

        PASS_A = [(t, h, n, (t + 1) * P) for t, n in ((0, 4), (1, 2), (2, 1), (3, 1)) for h in range(0, 4, n)]
        PASS_B = [(t, h, n, (NT - t) * P) for t, n in ((0, 1), (1, 1), (2, 2), (3, 4)) for h in range(0, 4, n)]
        NA, NB = len(PASS_A), len(PASS_B)

        vS_count, total = {}, [0] * 4
        for n in range(2 * G):
            total[n % 4] += 16
            vS_count[n] = total[n % 4]
            if n % NT < NT - 1:
                total[(n + 1) % 4] += 16

        LN1, LN2, LN3, LN4 = 0, 8, 32, 40

        def tile(t):
            return slice(1 + t * P, 1 + (t + 1) * P)

        block = ctx.enter_context(nc.Block())

        @block.tensor
        def _(pe):
            def transposes(bank, sources, n=None):
                for i, src in enumerate(sources):
                    mm = pe.transpose(bank[:, i * P:(i + 1) * P], src, ident)
                return mm

            def features(c, b, ready, count):
                bank = take(pe, ("xT", c), [(xT_ready, c + 1)])
                pe.wait_ge(ready, count)
                transposes(bank, [xM[:, 4 * b + t, :] for t in range(NT)]).then_inc(pe_xT, 1)

            def retention():
                for b in range(2):
                    features(b, b, x_loaded[b], 16)
                for b in range(2):
                    pe.wait_ge(xT_ready, b + 1)
                    for kind in range(4):
                        i = 4 * b + kind
                        bank = take(pe, ("qk1", i), [(qk1_scaled, i + 1)])
                        pe.matmul(bank[:], w_("qk1")[:, kind * P:(kind + 1) * P], hT[:, b, 1:S + 1],
                                  start=True, stop=True).then_inc(pe_qk1, 1)
                    for t in range(NT):
                        g = 4 * b + t
                        bank = take(pe, ("vg", g), [(gate_pre, g + 1)])
                        pe.matmul(bank[:], hT[:, b, tile(t)], w_("vg1"), start=True, stop=True).then_inc(pe_vg, 1)
                for b in range(2):
                    pe.wait_ge(qkT_ready, 2 * b + 2)
                    bank = take(pe, ("kM", b), [(kM_ready, b + 1)])
                    transposes(bank, [kT1[:, b, t * P:(t + 1) * P] for t in range(NT)]).then_inc(pe_kM, 1)

                def scores(g):
                    b, t = divmod(g, NT)
                    pe.wait_ge(qx_ready, g + 1)
                    for c in range(4):
                        bank = take(pe, ("sc", g, c), [(PT1_ready, 4 * g + c + 1)])
                        pe.matmul(bank[:], kT1[:, b, t * P:(t + 1) * P], qx1[:, 4 * c:4 * c + 4, :],
                                  start=True, stop=True).then_inc(pe_sc, 1)

                def outputs(g):
                    b, t = divmod(g, NT)
                    bank = take(pe, ("o1", g), [(on_ready, g + 1)])
                    if g == 0:
                        pe.wait_ge(ones_ready, 1)
                    if t:
                        pe.wait_ge(state_ready, 3 * b + t)
                        pe.matmul(bank[:, 0:VW], qT1[:, b, t * P:(t + 1) * P], state[:, b, :],
                                  start=True, stop=False, skip_group_check=True)
                    for h in range(H1):
                        if h % 4 == 0:
                            pe.wait_ge(PT1_ready, 4 * g + h // 4 + 1)
                        mm = pe.matmul(bank[:, 17 * h:17 * h + 17], PT1[:, g % 2, h, :], v1[:, g, h, :],
                                       start=(t == 0 and h == 0), stop=(h == H1 - 1), skip_group_check=True)
                    mm.then_inc(pe_o1, 1)
                    if t < NT - 1:
                        bank = take(pe, ("kv", g), [(state_ready, 3 * b + t + 1)])
                        if t == 0:
                            pe.wait_ge(kM_ready, b + 1)
                        pe.matmul(bank[:, 0:VW], kM1[:, g, :], v1[:, g, :, :].rearrange("p h d -> p (h d)"),
                                  start=True, stop=True).then_inc(pe_kv, 1)

                def project(g):
                    pe.wait_ge(y_ready, g + 1)
                    bank = take(pe, ("yT", g), [(yT_ready, g + 1)])
                    transposes(bank, [y1[:, g % 2, 0:P], y1[:, g % 2, P:2 * P]]).then_inc(pe_yT, 1)
                    bank = take(pe, ("wo1", g), [(z1_ready, g + 1)])
                    pe.wait_ge(yT_ready, g + 1)
                    for k in range(2):
                        mm = pe.matmul(bank[:, 0:P], yT1[:, g % 2, k * P:(k + 1) * P],
                                       w_("wo1")[:, k * P:(k + 1) * P], start=(k == 0), stop=(k == 1))
                    mm.then_inc(pe_wo1, 1)

                for s in range(G + 3):
                    if s < G:
                        scores(s)
                    if 1 <= s <= G:
                        outputs(s - 1)
                    if s >= 3:
                        project(s - 3)

            def window_layer(l):
                src = xM if l == 0 else xi
                for s in range(G + 3):
                    g = s - 1
                    if 0 <= g < G:
                        n = G * l + g
                        pe.wait_ge(rot_ready, n + 1)
                        bank = take(pe, ("qT", n), [(qT_ready, n + 1)])
                        transposes(bank, [qk2[:, g % 2, i * P:(i + 1) * P] for i in range(4)]).then_inc(pe_qT, 1)
                        bank = take(pe, ("kT", n), [(kz_ready, n + 1)])
                        transposes(bank, [qk2[:, g % 2, 512 + i * P:512 + (i + 1) * P] for i in range(4)])\
                            .then_inc(pe_kT, 1)
                    g = s
                    if g < G:
                        n = G * l + g
                        b, t = divmod(g, NT)
                        if t == 0:
                            i = 4 * l + b
                            bank = take(pe, ("hT", i), [(hT_ready, i + 1)])
                            if l == 0:
                                pe.wait_ge(xM_ready, NT * (b + 1))
                            else:
                                pe.wait_ge(xf_ready, NT * (b + 1))
                            transposes(bank, [src[:, 4 * b + j, :] for j in range(NT)]).then_inc(pe_hT, 1)
                            pe.wait_ge(hT_ready, i + 1)
                        for j, (name, done, until) in enumerate((("q", pe_q, (qn_ready, 2 * n + 1)),
                                                                 ("k", pe_k, (qn_ready, 2 * n + 2)),
                                                                 ("v", pe_v, (vA_ready, n + 1)))):
                            bank = take(pe, (name, n), [until])
                            pe.matmul(bank[:], hT[:, b, t * P:(t + 1) * P], w_(f"qkv2_{l}")[:, 512 * j:512 * j + 512],
                                      start=True, stop=True).then_inc(done, 1)
                    g = s - 2
                    if 0 <= g < G:
                        n = G * l + g
                        pe.wait_ge(P_ready, n + 1)
                        for c in range(2):
                            bank = take(pe, ("PT", n, c), [(PT2_ready, 2 * n + c + 1)])
                            transposes(bank, [sm2[:, g % 2, 4 * c + i, :] for i in range(4)]).then_inc(pe_PT, 1)
                    g = s - 1
                    if 0 <= g < G:
                        n = G * l + g
                        pe.wait_ge(qT_ready, n + 1)
                        pe.wait_ge(kz_ready, n + 1)
                        for c in range(2):
                            bank = take(pe, ("S", n, c), [(sm_ready, 2 * n + c + 1)])
                            for i in range(4):
                                h = 4 * c + i
                                for w in range(2):
                                    mm = pe.matmul(bank[64 * w:64 * w + 64, i * P:(i + 1) * P],
                                                   qT2[:, g % 2, h // 2, 64 * w:64 * w + 64],
                                                   kz[:, g % 2, h, 64 * w:64 * w + P], start=True, stop=True)
                            mm.then_inc(pe_S, 1)
                    g = s - 3
                    if 0 <= g < G:
                        n = G * l + g
                        pe.wait_ge(o_ready, 2 * n + 2)
                        bank = take(pe, ("oT", n), [(oT_ready, n + 1)])
                        transposes(bank, [o2[:, g % 2, 2 * i:2 * i + 2, :].rearrange("p h d -> p (h d)")
                                          for i in range(4)]).then_inc(pe_oT, 1)
                    g = s - 2
                    if 0 <= g < G:
                        n = G * l + g
                        pe.wait_ge(vA_ready, n + 1)
                        pe.wait_ge(vS_landed[n % 4], vS_count[n])
                        for c in range(2):
                            pe.wait_ge(PT2_ready, 2 * n + c + 1)
                            bank = take(pe, ("O", n, c), [(o_ready, 2 * n + c + 1)])
                            for i in range(4):
                                h = 4 * c + i
                                for w, v in ((0, vS2), (1, vA2)):
                                    mm = pe.matmul(bank[64 * w:64 * w + 64, 65 * i:65 * i + 65],
                                                   PT2[:, g % 2, h, 64 * w:64 * w + 64], v[:, n % 4, h, :],
                                                   start=True, stop=True)
                            mm.then_inc(pe_O, 1)
                    g = s - 3
                    if 0 <= g < G:
                        n = G * l + g
                        bank = take(pe, ("wo2", n), [(xa_ready, n + 1)])
                        pe.wait_ge(oT_ready, n + 1)
                        for k in range(4):
                            mm = pe.matmul(bank[:, 0:P], oT2[:, g % 2, k, :],
                                           w_(f"wo2_{l}")[:, k * P:(k + 1) * P], start=(k == 0), stop=(k == 3))
                        mm.then_inc(pe_wo2, 1)

            def gelu_layer(l):
                for g in range(G):
                    n = G * l + g
                    pe.wait_ge(xa_ready, n + 1)
                    bank = take(pe, ("hs", n), [(hn_ready, n + 1)])
                    mm = pe.matmul(bank[:, 0:64], c_("shift"), xi[:, g, 64:P], start=True, stop=(g % NT == 0))
                    if g % NT:
                        mm = pe.matmul(bank[:, 0:64], c_("carry"), xi[:, g - 1, 64:P], start=False, stop=True)
                    mm.then_inc(pe_hs, 1)
                    if g >= 1:
                        normed(l, g - 1)
                normed(l, G - 1)
                for b in range(2):
                    pe.wait_ge(hT_ready, 4 * l + 2 + b + 1)
                    for kb, K in enumerate(KB):
                        i = 3 * (2 * l + b) + kb
                        for name, at, done, until in (("wg", HID, pe_wg, gel_ready), ("wa", 0, pe_wa, hh_ready)):
                            bank = take(pe, (name, i), [(until, i + 1)])
                            pe.matmul(bank[0:K, :], w_(f"w1_{l}")[:, at + kb * P:at + kb * P + K],
                                      hT[:, b, 1:S + 1], start=True, stop=True).then_inc(done, 1)
                for g in range(G):
                    n = G * l + g
                    b, t = divmod(g, NT)
                    if t == 0:
                        pe.wait_ge(hh_ready, 3 * (2 * l + b) + 3)
                    bank = take(pe, ("w2", n), [(xf_ready, n + 1)])
                    for kb, K in enumerate(KB):
                        mm = pe.matmul(bank[:, 0:P], hh2[0:K, b, kb, t * P:(t + 1) * P],
                                       w_(f"w2_{l}")[0:K, kb * P:(kb + 1) * P], start=(kb == 0), stop=(kb == 2))
                    mm.then_inc(pe_w2, 1)

            def normed(l, g):
                n = G * l + g
                b, t = divmod(g, NT)
                i = 4 * l + 2 + b
                if t == 0:
                    take(pe, ("hT", i), [(hT_ready, i + 1)], bank=7)
                pe.wait_ge(hn_ready, n + 1)
                mm = pe.transpose(held(("hT", i))[:, t * P:(t + 1) * P], hn2[:, g % 2, :], ident)
                mm.then_inc(pe_hT, 1)

            def causal():
                for b in range(2):
                    features(2 + b, b, xM_ready, G + NT * (b + 1))
                for g in range(G):
                    b, t = divmod(g, NT)
                    pe.wait_ge(xT_ready, 2 + b + 1)
                    bank = take(pe, ("qkv3", g), [(v3_ready, g + 1)])
                    pe.matmul(bank[:, 0:384], hT[:, b, tile(t)], w_("qkv3"), start=True, stop=True)\
                        .then_inc(pe_qkv3, 1)

                def strips(u):
                    b, quad = divmod(u, 4)
                    pe.wait_ge(strips_ready, NT * (b + 1))
                    for name, src, done, until in (
                            ("qS", QS, pe_qS, [(qS_ready, u + 1)]),
                            ("kS", KS, pe_kS, [(kxd_ready, u + 1)])):
                        bank = take(pe, (name, u), until)
                        transposes(bank, [src[:, 4 * b + t, 4 * quad:4 * quad + 4, :].rearrange("p h r -> p (h r)")
                                          for t in range(NT)]).then_inc(done, 1)

                def pass_a(u):
                    pe.wait_ge(qS_ready, u + 1)
                    pe.wait_ge(kxa_ready, u + 1)
                    pe.wait_ge(kxd_ready, u + 1)
                    for j, (t, h, n, wide) in enumerate(PASS_A):
                        i = NA * u + j
                        bank = take(pe, ("A", i), [(mx_ready, i + 1)])
                        view = bank[:, 0:n * wide].rearrange("p (h j) -> p h j", h=n)
                        pe.matmul(view, qS[:, u % 2, t * P:(t + 1) * P], kx[:, u % 2, h:h + n, 0:wide],
                                  start=True, stop=False, skip_group_check=True)
                        pe.matmul(view[:, :, wide - P:wide], ident_bf[:],
                                  mask_ij[:].unsqueeze(1).to_broadcast([P, n, P]),
                                  start=False, stop=True, skip_group_check=True).then_inc(pe_A, 1)

                def strips_shifted(u):
                    b, quad = divmod(u, 4)
                    pe.wait_ge(negmax_ready, u + 1)
                    bank = take(pe, ("qS2", u), [(qS2_ready, u + 1)])
                    transposes(bank, [QS[:, 4 * b + t, 4 * quad:4 * quad + 4, :].rearrange("p h r -> p (h r)")
                                      for t in range(NT)]).then_inc(pe_qS2, 1)

                def pass_b(u, j):
                    t, h, n, wide = PASS_B[j]
                    i = NB * u + j
                    bank = take(pe, ("B", i), [(E_ready, i + 1)])
                    for k in range(n):
                        pe.matmul(bank[:, k * wide:(k + 1) * wide], kx[:, u % 2, h + k, t * P:(t + 1) * P],
                                  qS2[:, u % 2, t * P:S], start=(k == 0), stop=False, skip_group_check=True)
                    view = bank[:, 0:n * wide].rearrange("p (h j) -> p h j", h=n)
                    pe.matmul(view[:, :, 0:P], ident_bf[:], mask_ji[:].unsqueeze(1).to_broadcast([P, n, P]),
                              start=False, stop=True, skip_group_check=True).then_inc(pe_B, 1)

                def values(u, j):
                    b, quad = divmod(u, 4)
                    t, h, n, wide = PASS_B[j]
                    i = NB * u + j
                    if j == 0:
                        take(pe, ("o3", u), [(oS_ready, u + 1)], bank=7)
                        pe.wait_ge(v3_ready, NT * (b + 1))
                    pe.wait_ge(E_ready, i + 1)
                    for k in range(n):
                        mm = pe.matmul(psum[7][32 * (h + k):32 * (h + k) + 32, t * P:S],
                                       vp[:, 4 * b + t, 4 * quad + h + k, :],
                                       PT3[:, i % NSLOT, k * wide:(k + 1) * wide],
                                       start=(t == 0), stop=(t == NT - 1), skip_group_check=True)
                    mm.then_inc(pe_V, 1)

                def head_outputs(u):
                    bank = take(pe, ("oS", u), [(oN_ready, u + 1)])
                    pe.wait_ge(oS_ready, u + 1)
                    transposes(bank, [oS3[:, t * P:(t + 1) * P] for t in range(NT)]).then_inc(pe_oS, 1)

                LAG = 3
                for s in range(G + 1):
                    if s < G:
                        strips(s)
                    if s >= 1:
                        strips_shifted(s - 1)
                    if s < G:
                        pass_a(s)
                    if s >= 1:
                        pe.wait_ge(qS2_ready, s)
                        for j in range(NB + LAG):
                            if j < NB:
                                pass_b(s - 1, j)
                            if j >= LAG:
                                values(s - 1, j - LAG)
                        head_outputs(s - 1)
                for b in range(2):
                    pe.wait_ge(oN_ready, 4 * (b + 1))
                    bank = take(pe, ("oN", b), [(oNT_ready, b + 1)])
                    transposes(bank, [oN3[:, 4 * b + t, :, :].rearrange("p h d -> p (h d)") for t in range(NT)])\
                        .then_inc(pe_oN, 1)
                for g in range(G):
                    b, t = divmod(g, NT)
                    pe.wait_ge(oNT_ready, b + 1)
                    bank = take(pe, ("wo3", g), [(z3_ready, g + 1)])
                    pe.matmul(bank[:, 0:P], hT[:, b, tile(t)], w_("wo3"), start=True, stop=True).then_inc(pe_wo3, 1)

            def mlp():
                for b in range(2):
                    features(4 + b, b, xM_ready, 2 * G + NT * (b + 1))
                for b in range(2):
                    pe.wait_ge(xT_ready, 4 + b + 1)
                    for k in range(4):
                        i = 4 * b + k
                        for name, done, until in (("f1", pe_f1, silu_ready), ("f2", pe_f2, h0_ready)):
                            bank = take(pe, (name, i), [(until, i + 1)])
                            pe.matmul(bank[:], w_(name)[:, k * P:(k + 1) * P], hT[:, b, 1:S + 1],
                                      start=True, stop=True).then_inc(done, 1)
                for name, src, have, done, until in (("h1", h04, h0_ready, pe_h1, h1_ready),
                                                     ("h2", h14, h1_ready, pe_h2, h2_ready)):
                    for b in range(2):
                        pe.wait_ge(have, 4 * (b + 1))
                        for k in range(4):
                            i = 4 * b + k
                            bank = take(pe, (name, i), [(until, i + 1)])
                            for c in range(4):
                                mm = pe.matmul(bank[:], w_(name)[:, 512 * c + k * P:512 * c + (k + 1) * P],
                                               src[:, b, c, :], start=(c == 0), stop=(c == 3))
                            mm.then_inc(done, 1)
                for g in range(G):
                    b, t = divmod(g, NT)
                    pe.wait_ge(h2_ready, 4 * (b + 1))
                    bank = take(pe, ("w3", g), [(z4_scaled, g + 1)])
                    for c in range(4):
                        mm = pe.matmul(bank[:, 0:P], h04[:, b, c, t * P:(t + 1) * P], w_("w3")[:, c * P:(c + 1) * P],
                                       start=(c == 0), stop=(c == 3))
                    mm.then_inc(pe_w3, 1)

            pe.wait_ge(consts_loaded, 16)
            for s in loaded:
                pe.wait_ge(s, 16)
            pe.wait_ge(tables_ready, 2)
            with pe.Fori(0, 2) as it:
                retention()
                phase_end(pe, 1)
                for l in range(2):
                    if l == 0:
                        pe.wait_ge(pads_ready, 1)
                    window_layer(l)
                    gelu_layer(l)
                phase_end(pe, 2)
                pe.wait_ge(strips_blank, 2)
                causal()
                phase_end(pe, 3)
                mlp()
                pair_end(pe, it)

        @block.vector
        def _(dve):
            steps = [0]

            def link(ins):
                steps[0] += 1
                ins.then_inc(dve_step, 1)
                dve.wait_ge(dve_step, steps[0])

            def norm_stats(k, parts):
                for i, part in enumerate(parts):
                    link(dve.bn_stats(stats[:, 6 * i:6 * i + 6], part))
                link(dve.bn_aggr(meanvar[:, k % 4, :], stats[:, 0:6 * len(parts)]))
                dve.tensor_scalar(vareps[:, k % 4:k % 4 + 1], meanvar[:, k % 4, 1:2], EPS, None, ALU.add)\
                    .then_inc(var_ready, 1)

            def norm_apply(k, dst, src):
                dve.wait_ge(rstd_ready, k + 1)
                return dve.tensor_scalar(dst, src, meanvar[:, k % 4, 0:1], rstd[:, k % 4:k % 4 + 1],
                                         ALU.subtract, ALU.mult)

            def retention():
                dve.memset(v1[:, :, :, V1:V1 + 1], 1.0).then_inc(ones_ready, 1)
                for b in range(2):
                    for kind in range(4):
                        i = 4 * b + kind
                        if b:
                            dve.wait_ge(qkT_ready, kind // 2 + 1)
                        dve.wait_ge(pe_qk1, i + 1)
                        dve.scalar_tensor_tensor(out=scaled1[:, kind, :], in0=held(("qk1", i))[:],
                                                 scalar=w_("bqk1")[:, kind:kind + 1],
                                                 in1=c_("rot1")[:, kind * S:(kind + 1) * S],
                                                 op0=ALU.add, op1=ALU.mult).then_inc(qk1_scaled, 1)
                    for t in range(NT):
                        g = 4 * b + t
                        dve.wait_ge(pe_vg, g + 1)
                        dve.tensor_tensor(v1[:, g, :, 0:V1],
                                          held(("vg", g))[:, 0:256].rearrange("p (h d) -> p h d", h=H1),
                                          r_("bvg1")[:, 0:256].rearrange("p (h d) -> p h d", h=H1), ALU.add)
                        dve.tensor_tensor(gate1[:, g, :], held(("vg", g))[:, 256:512], r_("bvg1")[:, 256:512],
                                          ALU.add).then_inc(gate_pre, 1)

                def expand(g):
                    b, t = divmod(g, NT)
                    if g == 0 or g == NT:
                        dve.wait_ge(qkT_ready, 2 * b + 2)
                    if g:
                        dve.wait_ge(pe_sc, 4 * g)
                    dve.tensor_tensor(qx1[:], qT1[:, b:b + 1, t * P:(t + 1) * P].to_broadcast([P, H1, P]),
                                      c_("headmask").unsqueeze(2).to_broadcast([P, H1, P]), ALU.mult)\
                        .then_inc(qx_ready, 1)

                def masked(g):
                    if g >= 2:
                        dve.wait_ge(pe_o1, g - 1)
                    for c in range(4):
                        dve.wait_ge(pe_sc, 4 * g + c + 1)
                        dve.tensor_tensor(PT1[:, g % 2, 4 * c:4 * c + 4, :],
                                          held(("sc", g, c))[:].rearrange("p (h j) -> p h j", h=4),
                                          c_("causal1").unsqueeze(1).to_broadcast([P, 4, P]), ALU.mult)\
                            .then_inc(PT1_ready, 1)

                def update_state(g):
                    b, t = divmod(g, NT)
                    dve.wait_ge(pe_kv, 3 * b + t + 1)
                    tmp = a1["statetmp"]
                    if t == 0:
                        dve.tensor_tensor(state[:, b, :], held(("kv", g))[:, 0:VW], c_("statemask"), ALU.mult)\
                            .then_inc(state_ready, 1)
                    else:
                        link(dve.tensor_tensor(tmp, held(("kv", g))[:, 0:VW], c_("statemask"), ALU.mult))
                        dve.scalar_tensor_tensor(out=state[:, b, :], in0=state[:, b, :], scalar=c_("chunkdecay"),
                                                 in1=tmp, op0=ALU.mult, op1=ALU.add).then_inc(state_ready, 1)

                def normalise(g):
                    o = held(("o1", g))[:, 0:VW].rearrange("p (h d) -> p h d", h=H1)
                    total = o[:, :, V1:V1 + 1]
                    den, mu = a1["den"].unsqueeze(2), a1["mu"].unsqueeze(2)
                    dve.wait_ge(pe_o1, g + 1)
                    if g:
                        dve.wait_ge(gvar_ready, g)
                    link(dve.tensor_scalar(mu, total, -1.0, None, ALU.mult))
                    link(dve.tensor_tensor(den, total, mu, ALU.max))
                    link(dve.tensor_scalar(den, den, 1.0, None, ALU.max))
                    link(dve.reciprocal(den, den))
                    dve.tensor_tensor(on1[:], o[:, :, 0:V1], den.to_broadcast([P, H1, V1]), ALU.mult)\
                        .then_inc(on_ready, 1)
                    dve.wait_ge(on_ready, g + 1)
                    link(dve.tensor_reduce(a1["mu"], on1[:], AX, ALU.add))
                    link(dve.tensor_scalar(mu, mu, 1.0 / V1, None, ALU.mult))
                    if g >= 2:
                        dve.wait_ge(cg_ready, g - 1)
                    dve.tensor_tensor(cen1[:, g % 2], on1[:], mu.to_broadcast([P, H1, V1]), ALU.subtract)\
                        .then_inc(cen_ready, 1)
                    dve.wait_ge(cen_ready, g + 1)
                    link(dve.tensor_tensor(sq1[:], cen1[:, g % 2], cen1[:, g % 2], ALU.mult))
                    link(dve.tensor_reduce(a1["mu"], sq1[:], AX, ALU.add))
                    dve.tensor_scalar(gvar1[:, g % 2, :], a1["mu"], 1.0 / V1, EPS, ALU.mult, ALU.add)\
                        .then_inc(gvar_ready, 1)

                def gated(g):
                    dve.wait_ge(grstd_ready, g + 1)
                    dve.wait_ge(cg_ready, g + 1)
                    if g >= 2:
                        dve.wait_ge(pe_yT, g - 1)
                    dve.tensor_tensor(y1[:, g % 2, :].rearrange("p (h d) -> p h d", h=H1), cg1[:, g % 2],
                                      grstd1[:, g % 2, :].unsqueeze(2).to_broadcast([P, H1, V1]), ALU.mult)\
                        .then_inc(y_ready, 1)

                def residual(g):
                    dve.wait_ge(pe_wo1, g + 1)
                    dve.wait_ge(xb1_ready, 1)
                    if g >= 2:
                        dve.wait_ge(xM_ready, g - 1)
                    dve.tensor_tensor(z1[:, g % 2, :], held(("wo1", g))[:, 0:P], xi[:, g, :], ALU.add)\
                        .then_inc(z1_ready, 1)
                    dve.wait_ge(z1_ready, g + 1)
                    norm_stats(LN1 + g, [z1[:, g % 2, :]])

                expand(0)
                for s in range(G + 5):
                    if s < G:
                        masked(s)
                    if s + 1 < G:
                        expand(s + 1)
                    if 1 <= s <= G:
                        if (s - 1) % NT < NT - 1:
                            update_state(s - 1)
                        normalise(s - 1)
                    if 2 <= s <= G + 1:
                        gated(s - 2)
                    if 4 <= s:
                        if s - 4 < G:
                            residual(s - 4)
                        if s >= 5:
                            norm_apply(LN1 + s - 5, xM[:, s - 5, :], z1[:, (s - 5) % 2, :]).then_inc(xM_ready, 1)

            def window_layer(l):
                src = xM if l == 0 else xi
                for s in range(G + 3):
                    g = s
                    if g < G:
                        n = G * l + g
                        dve.wait_ge(sq_ready, 2 * n + 2)
                        link(dve.tensor_reduce(ss2[:, g % 2, :], sq2.rearrange("p (h d) -> p h d", d=D2),
                                               AX, ALU.add))
                        dve.tensor_scalar(ss2[:, g % 2, :], ss2[:, g % 2, :], 1e-24, None, ALU.max)\
                            .then_inc(ss_ready, 1)
                    g = s - 1
                    if 0 <= g < G:
                        n = G * l + g
                        if n >= 2:
                            dve.wait_ge(pe_PT, 2 * (n - 1))
                        band = c_("band_first" if g % NT == 0 else "band")
                        for c in range(2):
                            dve.wait_ge(pe_S, 2 * n + c + 1)
                            dve.tensor_tensor(sm2[:, g % 2, 4 * c:4 * c + 4, :],
                                              held(("S", n, c))[:].rearrange("p (h j) -> p h j", h=4),
                                              band.unsqueeze(1).to_broadcast([P, 4, P]), ALU.add)\
                                .then_inc(sm_ready, 1)
                        dve.wait_ge(sm_ready, 2 * n + 2)
                        link(dve.tensor_reduce(a2["mx"], sm2[:, g % 2], AX, ALU.max))
                        dve.tensor_tensor(sm2[:, g % 2], sm2[:, g % 2],
                                          a2["mx"].unsqueeze(2).to_broadcast([P, H2, P]), ALU.subtract)\
                            .then_inc(smx_ready, 1)
                    g = s
                    if g < G:
                        n = G * l + g
                        t = g % NT
                        if n >= 2:
                            dve.wait_ge(pe_kT, n - 1)
                        dve.wait_ge(rn_ready, n + 1)
                        for i, name in enumerate("qk"):
                            dve.tensor_tensor(
                                qk2[:, g % 2, 512 * i:512 * i + 512].rearrange("p (h d) -> p h d", h=H2),
                                held((name, n))[:].rearrange("p (h d) -> p h d", h=H2),
                                rn2[:, g % 2, H2 * i:H2 * i + H2].unsqueeze(2).to_broadcast([P, H2, D2]),
                                ALU.mult).then_inc(qn_ready, 1)
                        dve.wait_ge(qn_ready, 2 * n + 2)
                        if n:
                            dve.wait_ge(rot_ready, n)
                        heads = qk2[:, g % 2, :].rearrange("p (i h d) -> p i h d", i=2, h=H2)
                        swap = swapped2.rearrange("p (i h d) -> p i h d", i=2, h=H2)
                        for half in range(2):
                            a, z = 32 * half, 32 * (1 - half)
                            dve.tensor_tensor(swap[:, :, :, a:a + 32], heads[:, :, :, z:z + 32],
                                              table2[:, l, 1, t, :, a:a + 32].unsqueeze(2)
                                              .to_broadcast([P, 2, H2, 32]), ALU.mult).then_inc(swapped_ready, 1)
                    g = s - 2
                    if 0 <= g < G:
                        n = G * l + g
                        if n >= 2:
                            dve.wait_ge(pe_oT, n - 1)
                        for c in range(2):
                            dve.wait_ge(pe_O, 2 * n + c + 1)
                            o = held(("O", n, c))[:, 0:260].rearrange("p (h d) -> p h d", h=4)
                            rs = a2["rs"][:, 4 * c:4 * c + 4].unsqueeze(2)
                            link(dve.reciprocal(rs, o[:, :, D2:D2 + 1]))
                            dve.tensor_tensor(o2[:, g % 2, 4 * c:4 * c + 4, :], o[:, :, 0:D2],
                                              rs.to_broadcast([P, 4, D2]), ALU.mult).then_inc(o_ready, 1)
                    g = s - 3
                    if 0 <= g < G:
                        n = G * l + g
                        dve.wait_ge(pe_wo2, n + 1)
                        dve.tensor_tensor(xi[:, g, :], held(("wo2", n))[:, 0:P], src[:, g, :], ALU.add)\
                            .then_inc(xa_ready, 1)

            def gelu_layer(l):
                first = LN2 + G * l

                def apply(g):
                    n = G * l + g
                    if n >= 2:
                        dve.wait_ge(pe_hT, hn_seen(n - 2))
                    norm_apply(first + g, hn2[:, g % 2, 0:64], xi[:, g, 0:64])
                    norm_apply(first + g, hn2[:, g % 2, 64:P], held(("hs", n))[:, 0:64]).then_inc(hn_ready, 1)

                for g in range(G):
                    n = G * l + g
                    dve.wait_ge(xa_ready, n + 1)
                    dve.wait_ge(pe_hs, n + 1)
                    norm_stats(first + g, [xi[:, g, 0:64], held(("hs", n))[:, 0:64]])
                    if g >= 1:
                        apply(g - 1)
                apply(G - 1)
                for b in range(2):
                    for kb, K in enumerate(KB):
                        i = 3 * (2 * l + b) + kb
                        dve.wait_ge(gel_ready, i + 1)
                        dve.wait_ge(pe_wa, i + 1)
                        dve.scalar_tensor_tensor(out=hh2[0:K, b, kb, :], in0=held(("wa", i))[0:K, :],
                                                 scalar=w_(f"b1_{l}")[0:K, kb:kb + 1], in1=gel2[0:K, i % 2, :],
                                                 op0=ALU.add, op1=ALU.mult).then_inc(hh_ready, 1)
                last_norm = LN2 + 2 * G
                dve.wait_ge(xb2_ready, l + 1)
                for g in range(G):
                    n = G * l + g
                    dve.wait_ge(pe_w2, n + 1)
                    dve.tensor_tensor(xi[:, g, :], held(("w2", n))[:, 0:P], xi[:, g, :], ALU.add)\
                        .then_inc(xf_ready, 1)
                    if l == 1:
                        dve.wait_ge(xf_ready, n + 1)
                        norm_stats(last_norm + g, [xi[:, g, :]])
                        if g >= 1:
                            norm_apply(last_norm + g - 1, xM[:, g - 1, :], xi[:, g - 1, :]).then_inc(xM_ready, 1)
                if l == 1:
                    norm_apply(last_norm + G - 1, xM[:, G - 1, :], xi[:, G - 1, :]).then_inc(xM_ready, 1)

            def causal():
                def stats3(g):
                    bank = held(("qkv3", g))[:, 0:256].rearrange("p (h d) -> p h d", h=32)
                    dve.wait_ge(pe_qkv3, g + 1)
                    if g:
                        dve.wait_ge(var3_ready, g)
                    mu = a3["mu"]
                    link(dve.tensor_reduce(mu, bank, AX, ALU.add))
                    link(dve.tensor_scalar(mu, mu, 1.0 / D3, None, ALU.mult))
                    dve.tensor_tensor(cen3[:, g % 2], bank, mu.unsqueeze(2).to_broadcast([P, 32, D3]),
                                      ALU.subtract).then_inc(cen3_ready, 1)
                    dve.wait_ge(cen3_ready, g + 1)
                    link(dve.tensor_tensor(sq3[:], cen3[:, g % 2], cen3[:, g % 2], ALU.mult))
                    link(dve.tensor_reduce(mu, sq3[:], AX, ALU.add))
                    dve.tensor_scalar(var3[:, g % 2, :], mu, 1.0 / D3, EPS, ALU.mult, ALU.add)\
                        .then_inc(var3_ready, 1)

                def cut(g):
                    dve.wait_ge(rs3_ready, g + 1)
                    if g:
                        dve.wait_ge(strips_ready, g)
                    link(dve.tensor_tensor(n3[:], cen3[:, g % 2],
                                           rs3[:, g % 2, :].unsqueeze(2).to_broadcast([P, 32, D3]), ALU.mult))
                    link(dve.tensor_tensor(n3[:], n3[:], r_("g3").rearrange("p (h d) -> p h d", h=32), ALU.mult))
                    link(dve.tensor_tensor(n3[:], n3[:], r_("b3").rearrange("p (h d) -> p h d", h=32), ALU.add))
                    link(dve.tensor_copy(hi3[:], n3[:].rearrange("p h d -> p (h d)")))
                    hi = hi3[:].bitcast(F32).rearrange("p (h d) -> p h d", h=32)
                    if g == 0:
                        dve.wait_ge(strips_blank, 2)
                    dve.tensor_copy(QS[:, g, :, 0:8], hi[:, 0:16, :])
                    dve.tensor_copy(QS[:, g, :, 8:16], hi[:, 0:16, :])
                    dve.tensor_copy(KS[:, g, :, 0:8], hi[:, 16:32, :])
                    dve.tensor_copy(KS[:, g, :, 16:24], hi[:, 16:32, :])
                    dve.tensor_tensor(QS[:, g, :, 16:24], n3[:, 0:16, :], hi[:, 0:16, :], ALU.subtract)
                    dve.tensor_tensor(KS[:, g, :, 8:16], n3[:, 16:32, :], hi[:, 16:32, :], ALU.subtract)\
                        .then_inc(strips_ready, 1)

                for g in range(G + 1):
                    if g < G:
                        stats3(g)
                    if g >= 1:
                        cut(g - 1)

                def kstrips(u):
                    dve.wait_ge(kxa_ready, u + 1)
                    if u >= 2:
                        dve.wait_ge(pe_B, NB * (u - 1))
                    for h in (2, 3):
                        ins = dve.tensor_copy(kx[32 * h:32 * h + 32, u % 2, h, :],
                                              held(("kS", u))[32 * h:32 * h + 32, :])
                    ins.then_inc(kxd_ready, 1)

                def maxima(u):
                    b, quad = divmod(u, 4)
                    for j, (t, h, n, wide) in enumerate(PASS_A):
                        i = NA * u + j
                        dve.wait_ge(pe_A, i + 1)
                        dve.tensor_reduce(mx3[:, u % 2, t, h:h + n],
                                          held(("A", i))[:, 0:n * wide].rearrange("p (h j) -> p h j", h=n),
                                          AX, ALU.max).then_inc(mx_ready, 1)
                    dve.wait_ge(mx_ready, NA * (u + 1))
                    mx = mx3[:, u % 2]
                    if u:
                        dve.wait_ge(negmax_ready, u)
                    neg = neg3[:].bitcast(F32).rearrange("p (t h) -> p t h", t=NT)
                    link(dve.tensor_scalar(neg3[:].rearrange("p (t h) -> p t h", t=NT), mx, -1.0, None, ALU.mult))
                    dst = QS[:, 4 * b:4 * b + 4, 4 * quad:4 * quad + 4, :]
                    dve.tensor_copy(dst[:, :, :, 24], neg)
                    dve.scalar_tensor_tensor(out=dst[:, :, :, 25], in0=mx, scalar=-1.0, in1=neg,
                                             op0=ALU.mult, op1=ALU.subtract).then_inc(negmax_ready, 1)

                def weighted(u):
                    b, quad = divmod(u, 4)
                    dve.wait_ge(pe_oS, u + 1)
                    o = held(("oS", u))[:].rearrange("p (t h r) -> p t h r", t=NT, h=4)
                    link(dve.reciprocal(r3[:], o[:, :, :, D3]))
                    dve.tensor_tensor(oN3[:, 4 * b:4 * b + 4, 4 * quad:4 * quad + 4, :], o[:, :, :, 0:D3],
                                      r3[:].unsqueeze(3).to_broadcast([P, NT, 4, D3]), ALU.mult)\
                        .then_inc(oN_ready, 1)

                for s in range(G + 2):
                    if s < G:
                        kstrips(s)
                    if s >= 2:
                        weighted(s - 2)
                    if s < G:
                        maxima(s)
                for g in range(G):
                    dve.wait_ge(pe_wo3, g + 1)
                    dve.wait_ge(xb3_ready, 1)
                    if g >= 2:
                        dve.wait_ge(xM_ready, 2 * G + g - 1)
                    dve.tensor_tensor(z3[:, g % 2, :], held(("wo3", g))[:, 0:P], xi[:, g, :], ALU.add)\
                        .then_inc(z3_ready, 1)
                    dve.wait_ge(z3_ready, g + 1)
                    norm_stats(LN3 + g, [z3[:, g % 2, :]])
                    if g >= 1:
                        norm_apply(LN3 + g - 1, xM[:, g - 1, :], z3[:, (g - 1) % 2, :]).then_inc(xM_ready, 1)
                norm_apply(LN3 + G - 1, xM[:, G - 1, :], z3[:, (G - 1) % 2, :]).then_inc(xM_ready, 1)

            def mlp():
                for i in range(2 * 4):
                    b, k = divmod(i, 4)
                    dve.wait_ge(silu_ready, i + 1)
                    dve.wait_ge(pe_f2, i + 1)
                    dve.scalar_tensor_tensor(out=h04[:, b, k, :], in0=held(("f2", i))[:],
                                             scalar=w_("s4")[:, 4 + k:5 + k], in1=silu4[:, i % 2, :],
                                             op0=ALU.mult, op1=ALU.mult).then_inc(h0_ready, 1)
                for g in range(G):
                    dve.wait_ge(pe_w3, g + 1)
                    dve.tensor_tensor(t4[:, g % 2, :], held(("w3", g))[:, 0:P], r_("s3"), ALU.mult)\
                        .then_inc(z4_scaled, 1)
                    dve.wait_ge(z4_scaled, g + 1)
                    if g >= 2:
                        dve.wait_ge(out_ready, g - 1)
                    link(dve.tensor_tensor(z4[:, g % 2, :], t4[:, g % 2, :], xM[:, g, :], ALU.add))
                    norm_stats(LN4 + g, [z4[:, g % 2, :]])
                    if g >= 1:
                        norm_apply(LN4 + g - 1, xi[:, g - 1, :], z4[:, (g - 1) % 2, :]).then_inc(out_ready, 1)
                norm_apply(LN4 + G - 1, xi[:, G - 1, :], z4[:, (G - 1) % 2, :]).then_inc(out_ready, 1)

            dve.memset(neghalf[:], -0.5)
            dve.memset(hT[64:P, :, 0:1], 0.0)
            dve.wait_ge(consts_loaded, 16)
            dve.tensor_copy(mask_ij[:], c_("mask_ij"))
            dve.tensor_copy(mask_ji[:], c_("mask_ji"))
            dve.tensor_copy(ident_bf[:], ident)
            for s in loaded:
                dve.wait_ge(s, 16)
            rot2 = c_("rot2").rearrange("p (k t d) -> p k t d", k=4, t=NT)
            for l in range(2):
                gains = r_(f"qs{l}").rearrange("p (k d) -> p k d", k=4)
                for k in range(4):
                    dve.tensor_tensor(table2[:, l, k % 2, :, k // 2, :], rot2[:, k, :, :],
                                      gains[:, k:k + 1, :].to_broadcast([P, NT, D2]), ALU.mult)
            for name in ("g3", "b3"):
                ins = dve.tensor_scalar(r_(name), r_(name), float(D) ** -0.25, None, ALU.mult)
            dve.drain().then_inc(tables_ready, 1)
            dve.wait_ge(tables_ready, 1)
            with dve.Fori(0, 2) as it:
                retention()
                phase_end(dve, 1)
                for l in range(2):
                    window_layer(l)
                    gelu_layer(l)
                phase_end(dve, 2)
                causal()
                phase_end(dve, 3)
                mlp()
                pair_end(dve, it)

        @block.scalar
        def _(act):
            def evac(dst, src):
                return act.activation(dst, src, ACT.Copy)

            def features(c, b):
                act.wait_ge(pe_xT, c + 1)
                evac(hT[:, b, 1:S + 1], held(("xT", c))[:]).then_inc(xT_ready, 1)

            def retention():
                for b in range(2):
                    features(b, b)
                for g in range(G):
                    act.wait_ge(gate_pre, g + 1)
                    act.activation(gate1[:, g, :], gate1[:, g, :], ACT.Silu).then_inc(gate_ready, 1)
                for b in range(2):
                    act.wait_ge(pe_kM, b + 1)
                    evac(kM1[:, 4 * b:4 * b + 4, :].rearrange("p g d -> p (g d)"), held(("kM", b))[:])\
                        .then_inc(kM_ready, 1)
                for g in range(G):
                    act.wait_ge(pe_yT, g + 1)
                    if g >= 2:
                        act.wait_ge(pe_wo1, g - 1)
                    evac(yT1[:, g % 2, :], held(("yT", g))[:, 0:256]).then_inc(yT_ready, 1)

            def window_layer(l):
                for s in range(G + 3):
                    g = s - 1
                    if 0 <= g < G:
                        n = G * l + g
                        if n >= 2:
                            act.wait_ge(pe_S, 2 * (n - 1))
                        act.wait_ge(pe_qT, n + 1)
                        evac(qT2[:, g % 2].rearrange("p m d -> p (m d)"), held(("qT", n))[:]).then_inc(qT_ready, 1)
                        act.wait_ge(pe_kT, n + 1)
                        src = held(("kT", n))[:].rearrange("p (m d) -> p m d", m=4)
                        if n:
                            act.wait_ge(pe_S, 2 * n)
                        for half in range(2):
                            rows = slice(64 * half, 64 * half + 64)
                            ins = evac(kz[rows, g % 2, half:H2:2, 64:192], src[rows, :, :])
                            if g % NT < NT - 1:
                                ins = evac(kz[rows, (g + 1) % 2, half:H2:2, 0:64], src[rows, :, 64:P])
                        ins.then_inc(kz_ready, 1)
                    g = s
                    if g < G:
                        n = G * l + g
                        b, t = divmod(g, NT)
                        if t == 0:
                            i = 4 * l + b
                            act.wait_ge(pe_hT, (2 + G) * l + b + 1)
                            evac(hT[0:64, b, 0:S], held(("hT", i))[0:64, :])
                            evac(hT[64:P, b, 1:S + 1], held(("hT", i))[64:P, :]).then_inc(hT_ready, 1)
                        if n:
                            act.wait_ge(ss_ready, n)
                        for j, (name, done) in enumerate((("q", pe_q), ("k", pe_k))):
                            act.wait_ge(done, n + 1)
                            act.activation(sq2[:, 512 * j:512 * j + 512], held((name, n))[:], ACT.Square)\
                                .then_inc(sq_ready, 1)
                    g = s - 2
                    if 0 <= g < G:
                        n = G * l + g
                        if n >= 2:
                            act.wait_ge(pe_O, 2 * (n - 1))
                        for c in range(2):
                            act.wait_ge(pe_PT, 2 * n + c + 1)
                            evac(PT2[:, g % 2, 4 * c:4 * c + 4, :].rearrange("p h j -> p (h j)"),
                                 held(("PT", n, c))[:]).then_inc(PT2_ready, 1)
                    g = s
                    if g < G:
                        n = G * l + g
                        act.wait_ge(pe_v, n + 1)
                        if n >= 4:
                            act.wait_ge(pe_O, 2 * (n - 2))
                        evac(vA2[:, n % 4, :, 0:D2], held(("v", n))[:].rearrange("p (h d) -> p h d", h=H2))\
                            .then_inc(vA_ready, 1)
                    g = s - 3
                    if 0 <= g < G:
                        n = G * l + g
                        act.wait_ge(pe_oT, n + 1)
                        if n >= 2:
                            act.wait_ge(pe_wo2, n - 1)
                        evac(oT2[:, g % 2].rearrange("p m d -> p (m d)"), held(("oT", n))[:]).then_inc(oT_ready, 1)
                    g = s - 1
                    if 0 <= g < G:
                        n = G * l + g
                        act.wait_ge(smx_ready, n + 1)
                        act.activation(sm2[:, g % 2], sm2[:, g % 2], ACT.Exp).then_inc(P_ready, 1)

            def gelu_layer(l):
                for b in range(2):
                    i = 4 * l + 2 + b
                    act.wait_ge(pe_hT, (2 + G) * l + 2 + NT * (b + 1))
                    act.activation(hT[:, b, 1:S + 1], held(("hT", i))[:], ACT.Identity,
                                   bias=w_(f"ln2_{l}")[:, 1:2], scale=w_(f"ln2_{l}")[:, 0:1]).then_inc(hT_ready, 1)
                for b in range(2):
                    for kb, K in enumerate(KB):
                        i = 3 * (2 * l + b) + kb
                        act.wait_ge(pe_wg, i + 1)
                        if i >= 2:
                            act.wait_ge(hh_ready, i - 1)
                        act.activation(gel2[0:K, i % 2, :], held(("wg", i))[0:K, :], ACT.Gelu,
                                       bias=w_(f"b1_{l}")[0:K, 3 + kb:4 + kb], scale=1.0).then_inc(gel_ready, 1)

            def causal():
                for b in range(2):
                    features(2 + b, b)
                act.wait_ge(strips_blank, 2)
                for g in range(G):
                    act.wait_ge(cen3_ready, g + 1)
                    evac(vp[:, g, :, 0:D3], held(("qkv3", g))[:, 256:384].rearrange("p (h d) -> p h d", h=H3))\
                        .then_inc(v3_ready, 1)
                for s in range(G + 1):
                    u = s
                    if u < G:
                        act.wait_ge(pe_qS, u + 1)
                        if u >= 2:
                            act.wait_ge(pe_A, NA * (u - 1))
                        evac(qS[:, u % 2, :], held(("qS", u))[:]).then_inc(qS_ready, 1)
                        act.wait_ge(pe_kS, u + 1)
                        if u >= 2:
                            act.wait_ge(pe_B, NB * (u - 1))
                        for h in (0, 1):
                            ins = evac(kx[32 * h:32 * h + 32, u % 2, h, :], held(("kS", u))[32 * h:32 * h + 32, :])
                        ins.then_inc(kxa_ready, 1)
                    u = s - 1
                    if u >= 0:
                        act.wait_ge(pe_qS2, u + 1)
                        evac(qS2[:, u % 2, :], held(("qS2", u))[:]).then_inc(qS2_ready, 1)
                        for j, (t, h, n, wide) in enumerate(PASS_B):
                            i = NB * u + j
                            act.wait_ge(pe_B, i + 1)
                            if i >= NSLOT:
                                act.wait_ge(pe_V, i - NSLOT + 1)
                            act.activation(PT3[:, i % NSLOT, 0:n * wide], held(("B", i))[:, 0:n * wide], ACT.Exp)\
                                .then_inc(E_ready, 1)
                        act.wait_ge(pe_V, NB * (u + 1))
                        if u:
                            act.wait_ge(pe_oS, u)
                        evac(oS3, psum[7][:]).then_inc(oS_ready, 1)
                for b in range(2):
                    act.wait_ge(pe_oN, b + 1)
                    evac(hT[:, b, 1:S + 1], held(("oN", b))[:]).then_inc(oNT_ready, 1)

            def mlp():
                for b in range(2):
                    features(4 + b, b)
                for i in range(2 * 4):
                    act.wait_ge(pe_f1, i + 1)
                    if i >= 2:
                        act.wait_ge(h0_ready, i - 1)
                    act.activation(silu4[:, i % 2, :], held(("f1", i))[:], ACT.Silu,
                                   scale=w_("s4")[:, i % 4:i % 4 + 1]).then_inc(silu_ready, 1)
                for name, dst, done, ready, at in (("h1", h14, pe_h1, h1_ready, 8), ("h2", h04, pe_h2, h2_ready, 12)):
                    for i in range(2 * 4):
                        b, k = divmod(i, 4)
                        act.wait_ge(done, i + 1)
                        act.activation(dst[:, b, k, :], held((name, i))[:], ACT.Gelu,
                                       scale=w_("s4")[:, at + k:at + k + 1]).then_inc(ready, 1)

            for s in loaded:
                act.wait_ge(s, 16)
            act.wait_ge(tables_ready, 2)
            with act.Fori(0, 2) as it:
                retention()
                phase_end(act, 1)
                act.wait_ge(pads_ready, 1)
                for l in range(2):
                    window_layer(l)
                    gelu_layer(l)
                phase_end(act, 2)
                causal()
                phase_end(act, 3)
                mlp()
                pair_end(act, it)

        @block.gpsimd
        def _(pool):
            def root(k):
                pool.wait_ge(var_ready, k + 1)
                pool.tensor_tensor(rstd[:, k % 4:k % 4 + 1], vareps[:, k % 4:k % 4 + 1], neghalf[:], ALU.pow)\
                    .then_inc(rstd_ready, 1)

            def retention():
                for b in range(2):
                    pool.wait_ge(x_loaded[b], 16)
                pool.tensor_tensor(xi[:], xM[:], r_("bo1").unsqueeze(1).to_broadcast([P, G, D]), ALU.add)\
                    .then_inc(xb1_ready, 1)
                for b in range(2):
                    for side, dst in ((0, qT1), (1, kT1)):
                        pool.wait_ge(qk1_scaled, 4 * b + 2 * side + 2)
                        pool.tensor_tensor(dst[:, b, :], scaled1[:, 2 * side, :], scaled1[:, 2 * side + 1, :],
                                           ALU.add).then_inc(qkT_ready, 1)
                for s in range(G + 4):
                    g = s
                    if g < G:
                        pool.wait_ge(cen_ready, g + 1)
                        pool.wait_ge(gate_ready, g + 1)
                        if g >= 2:
                            pool.wait_ge(y_ready, g - 1)
                        pool.tensor_tensor(cg1[:, g % 2], cen1[:, g % 2],
                                           gate1[:, g, :].rearrange("p (h d) -> p h d", h=H1), ALU.mult)\
                            .then_inc(cg_ready, 1)
                        pool.wait_ge(gvar_ready, g + 1)
                        pool.tensor_tensor(grstd1[:, g % 2, :], gvar1[:, g % 2, :],
                                           neghalf[:].to_broadcast([P, H1]), ALU.pow).then_inc(grstd_ready, 1)
                    if s >= 3 and s - 3 < G:
                        root(LN1 + s - 3)

            def window_layer(l):
                for g in range(G):
                    n = G * l + g
                    t = g % NT
                    pool.wait_ge(ss_ready, n + 1)
                    pool.tensor_tensor(rn2[:, g % 2, :], ss2[:, g % 2, :], neghalf[:].to_broadcast([P, 16]), ALU.pow)\
                        .then_inc(rn_ready, 1)
                    pool.wait_ge(qn_ready, 2 * n + 2)
                    heads = qk2[:, g % 2, :].rearrange("p (i h d) -> p i h d", i=2, h=H2)
                    pool.tensor_tensor(straight2.rearrange("p (i h d) -> p i h d", i=2, h=H2), heads,
                                       table2[:, l, 0, t, :, :].unsqueeze(2).to_broadcast([P, 2, H2, D2]), ALU.mult)\
                        .then_inc(pool_step, 1)
                    pool.wait_ge(pool_step, n + 1)
                    pool.wait_ge(swapped_ready, 2 * n + 2)
                    pool.tensor_tensor(qk2[:, g % 2, :], straight2, swapped2, ALU.add).then_inc(rot_ready, 1)

            def gelu_layer(l):
                for g in range(G):
                    root(LN2 + G * l + g)
                pool.wait_ge(pe_hs, G * (l + 1))
                pool.wait_ge(hn_ready, G * (l + 1))
                ins = pool.tensor_tensor(xi[:], xi[:], r_(f"b2_{l}").unsqueeze(1).to_broadcast([P, G, D]), ALU.add)
                if l == 0:
                    ins.then_inc(xb2_ready, 1)
                else:
                    ins.then_inc(pool_step, 1)
                    pool.wait_ge(pool_step, 2 * G + 1)
                    pool.tensor_tensor(xi[:], xi[:], xM[:], ALU.add).then_inc(xb2_ready, 1)
                    for g in range(G):
                        root(LN2 + 2 * G + g)

            def causal():
                pool.memset(QS[:, :, :, 24:32], 0.0)
                pool.memset(KS[:, :, :, 24:26], 1.0)
                pool.memset(KS[:, :, :, 26:32], 0.0)
                pool.memset(vp[:, :, :, D3:D3 + 1], 1.0)
                pool.memset(vp[:, :, :, D3 + 1:32], 0.0)
                pool.drain().then_inc(strips_blank, 2)
                for g in range(G):
                    pool.wait_ge(var3_ready, g + 1)
                    pool.tensor_tensor(rs3[:, g % 2, :], var3[:, g % 2, :], neghalf[:].to_broadcast([P, 32]), ALU.pow)\
                        .then_inc(rs3_ready, 1)
                pool.tensor_tensor(xi[:], xM[:], r_("bo3").unsqueeze(1).to_broadcast([P, G, D]), ALU.add)\
                    .then_inc(xb3_ready, 1)
                for g in range(G):
                    root(LN3 + g)

            pool.memset(kx[:].bitcast(F32), 0.0)
            pool.wait_ge(tables_ready, 1)
            pool.drain().then_inc(tables_ready, 1)
            with pool.Fori(0, 2) as it:
                retention()
                phase_end(pool, 1)
                pool.memset(kz[:], 0.0)
                pool.memset(vS2[:], 0.0)
                pool.drain().then_inc(settle, 1)
                pool.memset(vS2[:, :, :, D2:D2 + 1], 1.0)
                pool.memset(vA2[:, :, :, D2:D2 + 1], 1.0)
                pool.drain().then_inc(pads_ready, 1)
                for l in range(2):
                    window_layer(l)
                    gelu_layer(l)
                phase_end(pool, 2)
                causal()
                phase_end(pool, 3)
                for g in range(G):
                    root(LN4 + g)
                pair_end(pool, it)

        @block.sync
        def _(sp):
            sp.dma_start(C[:], consts).then_inc(consts_loaded, 16)
            sp.dma_start(R[:], rows.to_broadcast([P, ROWS_WIDTH])).then_inc(loaded[0], 16)
            for i in range(1, 4):
                a, z = (0 if i == 1 else WEIGHT_CUTS[i]), WEIGHT_CUTS[i + 1]
                sp.dma_start(W[:, a:z], wts[:, a:z]).then_inc(loaded[i], 16)
            with sp.Fori(0, 2) as it:
                for b in range(2):
                    sp.dma_start(xM[:, 4 * b:4 * b + 4, :], x[2 * it + b].rearrange("(t p) d -> p t d", p=P))\
                        .then_inc(x_loaded[b], 16)
                sp.wait_ge(pads_ready, 1)
                for l in range(2):
                    for g in range(G):
                        n = G * l + g
                        sp.wait_ge(vA_ready, n + 1)
                        if n >= 4:
                            sp.wait_ge(pe_O, 2 * (n - 3))
                        sp.dma_start(vS2[64:P, n % 4, :, :], vA2[0:64, n % 4, :, :]).then_inc(vS_landed[n % 4], 16)
                        if g % NT < NT - 1:
                            if n >= 3:
                                sp.wait_ge(pe_O, 2 * (n - 2))
                            sp.dma_start(vS2[0:64, (n + 1) % 4, :, :], vA2[64:P, n % 4, :, :])\
                                .then_inc(vS_landed[(n + 1) % 4], 16)
                for g in range(G):
                    b, t = divmod(g, NT)
                    sp.wait_ge(out_ready, g + 1)
                    sp.dma_start(out[2 * it + b].rearrange("(t p) d -> p t d", p=P)[:, t, :], xi[:, g, :])\
                        .then_inc(stored, 16)
                sp.wait_ge(stored, 16 * G)
                sp.wait_ge(arrived, 4 * (it + 1))
                sp.sem_inc(settle)
                for s in cleared:
                    sp.sem_clear(s)
                sp.drain().then_inc(go, 1)


def _layout(inp):
    import numpy as np
    f = {k: np.asarray(v) for k, v in inp.items()}

    def swap(a):
        return a.reshape(a.shape[:-1] + (-1, 2))[..., ::-1].reshape(a.shape)

    def blocks(a):
        return a.reshape(-1, P, a.shape[-1]).transpose(1, 0, 2).reshape(P, -1)

    def padded(a):
        n = -(-a.shape[0] // P) * P
        return np.concatenate([a, np.zeros((n - a.shape[0],) + a.shape[1:], a.dtype)])

    def cols(*vs):
        return np.stack(vs, axis=1)

    w = {"qk1": np.concatenate([f["L0_attn_Wq"], swap(f["L0_attn_Wq"]), f["L0_attn_Wk"], swap(f["L0_attn_Wk"])], 1),
         "vg1": np.concatenate([f["L0_attn_Wv"], f["L0_attn_Wg"]], 1),
         "wo1": blocks(f["L0_attn_Wo"]),
         "bqk1": cols(f["L0_attn_bq"], swap(f["L0_attn_bq"]), f["L0_attn_bk"], swap(f["L0_attn_bk"])),
         "qkv3": np.concatenate([f["L1_attn_Wq"].T, f["L1_attn_Wk"].T, f["L1_attn_Wv"].T], 1),
         "wo3": f["L1_attn_Wo"].T,
         "f1": f["L1_ffn_w1_w"].T, "f2": f["L1_ffn_w2_w"].T, "h1": blocks(f["L1_ffn_h1_w"].T),
         "h2": blocks(f["L1_ffn_h2_w"].T), "w3": blocks(f["L1_ffn_w3_w"].T),
         "s4": np.concatenate([f[n].reshape(4, P).T for n in ("L1_ffn_w1_s", "L1_ffn_w2_s", "L1_ffn_h1_s",
                                                              "L1_ffn_h2_s")], 1)}
    for l in range(2):
        w[f"qkv2_{l}"] = f["L0_ffn_wqkv"][l]
        w[f"wo2_{l}"] = blocks(f["L0_ffn_wo"][l])
        w[f"w1_{l}"] = f["L0_ffn_w1"][l]
        w[f"w2_{l}"] = blocks(padded(f["L0_ffn_w2"][l]))
        b1 = f["L0_ffn_b1"][l]
        w[f"b1_{l}"] = np.concatenate([padded(b1[:HID]).reshape(3, P).T, padded(b1[HID:]).reshape(3, P).T], 1)
        w[f"ln2_{l}"] = cols(f["L0_ffn_ln_g"][l], f["L0_ffn_ln_b"][l])
    wts = np.ascontiguousarray(np.concatenate([w[n] for n in WEIGHTS], 1))

    def halves(a):
        return np.concatenate([a[32:], a[:32]])

    r = {"bvg1": np.concatenate([f["L0_attn_bv"], f["L0_attn_bg"]]), "bo1": f["L0_attn_bo"],
         "b2_0": f["L0_ffn_b2"][0], "b2_1": f["L0_ffn_b2"][1], "bo3": f["L1_attn_bo"], "s3": f["L1_ffn_w3_s"],
         "g3": np.concatenate([np.tile(f["L1_attn_qln_g"], H3), np.tile(f["L1_attn_kln_g"], H3)]),
         "b3": np.concatenate([np.tile(f["L1_attn_qln_b"], H3), np.tile(f["L1_attn_kln_b"], H3)])}
    for l in range(2):
        q, k = f["L0_ffn_q_scale"][l], f["L0_ffn_k_scale"][l]
        r[f"qs{l}"] = np.concatenate([q, halves(q), k, halves(k)])
    rows = np.ascontiguousarray(np.concatenate([r[n] for n in ROWS])[None, :])

    i = np.arange(P)
    pos = np.arange(S)
    f32 = np.float32
    c = {"ident": np.eye(P)}
    angle = np.repeat((1.0 / 10000.0 ** np.linspace(0.0, 1.0, K1 // 2, dtype=f32)).astype(f32), 2)
    turn = (pos[:, None].astype(f32) * angle[None, :]).astype(f32).astype(np.float64)
    gamma = 1.0 - 2.0 ** (-5.0 - np.arange(H1))
    dist = np.cumsum(gamma[:, None] ** pos[None, :], axis=1)
    local = pos % P
    qdecay = gamma[:, None] ** local[None, :] / np.sqrt(dist)
    kdecay = gamma[:, None] ** (-local[None, :]) * K1 ** -0.5
    sign = np.where(np.arange(K1) % 2 == 0, -1.0, 1.0)
    straight, swapped = np.cos(turn).T, (np.sin(turn) * sign).T
    c["rot1"] = np.concatenate([(d[:, None, :] * m[None, :, :]).reshape(D, S)
                                for d, m in ((qdecay, straight), (qdecay, swapped),
                                             (kdecay, straight), (kdecay, swapped))], 1)
    head = i // K1
    c["headmask"] = head[:, None] == np.arange(H1)[None, :]
    chunk = gamma[head] ** P
    c["statemask"] = np.repeat(c["headmask"], V1 + 1, axis=1) * chunk[:, None]
    c["chunkdecay"] = chunk[:, None]
    c["causal1"] = i[:, None] <= i[None, :]
    half = np.arange(0, D2, 2, dtype=f32)
    inv = (1.0 / 10000.0 ** (half / f32(D2))).astype(f32)
    fr = (pos[:, None].astype(f32) * inv[None, :]).astype(f32).astype(np.float64)
    fr = np.concatenate([fr, fr], 1)
    base = (half + 0.4 * D2) / (1.4 * D2)
    scale = base[None, :].astype(np.float64) ** ((pos - S // 2) / float(WIN // 2))[:, None]
    scale = np.concatenate([scale, scale], 1)
    sgn = np.where(np.arange(D2) < D2 // 2, -1.0, 1.0)
    tabs = [np.cos(fr) * scale * 8.0, np.sin(fr) * sgn * scale * 8.0, np.cos(fr) / scale, np.sin(fr) * sgn / scale]
    c["rot2"] = np.stack([t.reshape(NT, P, D2).transpose(1, 0, 2) for t in tabs], 1)
    q_, k_ = i[:, None] % WIN, i[None, :]
    allowed = (k_ >= q_) & (k_ <= q_ + WIN)
    c["band"] = np.where(allowed, 0.0, -1e30)
    c["band_first"] = np.where(allowed & ((i[:, None] >= WIN) | (k_ >= WIN)), 0.0, -1e30)
    c["mask_ij"] = np.where(i[None, :] > i[:, None], -1e30, 0.0)
    c["mask_ji"] = c["mask_ij"].T
    c["shift"] = i[None, :] == i[:, None] + 1
    c["carry"] = (i[:, None] == P - 1) & (i[None, :] == 0)
    consts = np.ascontiguousarray(np.concatenate([c[n].reshape(P, -1) for n in CONSTS], 1).astype(f32))
    return {"x": np.ascontiguousarray(f["L0_attn_x"]), "wts": wts, "rows": rows, "consts": consts}


def kernel(**inputs):
    import concourse.bacc as bacc
    from concourse.bass_utils import run_bass_kernel_spmd

    arrays = _layout(inputs)
    nc = bacc.Bacc("TRN2", target_bir_lowering=False, num_devices=1)
    args = [nc.dram_tensor(f"{n}_dram", a.shape, F32, kind="ExternalInput").ap() for n, a in arrays.items()]
    out = nc.dram_tensor("out_dram", arrays["x"].shape, F32, kind="ExternalOutput").ap()
    build(nc, *args, out)
    r = run_bass_kernel_spmd(nc, [{f"{n}_dram": a for n, a in arrays.items()}], core_ids=[0])
    return r.results[0]["out_dram"]
```

```python
from contextlib import ExitStack

import concourse.bass as bass
from concourse import mybir

ALU = mybir.AluOpType
ACT = mybir.ActivationFunctionType
F32 = mybir.dt.float32
F32R = mybir.dt.float32r
I32 = mybir.dt.int32
BF16 = mybir.dt.bfloat16
AX = mybir.AxisListType.X

P = 128
S = 512
NT = 4
G = 8
D = 128
H1, K1, V1 = 16, 8, 16
H2, D2, WIN = 8, 64, 64
HID = 341
KB = [128, 128, 85]
H3, D3 = 16, 8
EPS = 1e-5


def offsets(parts):
    at, out = 0, {}
    for name, width in parts:
        out[name] = (at, width)
        at += width
    return out, at


WEIGHTS, WEIGHTS_WIDTH = offsets(
    [("qk1", 4 * D), ("vg1", 512), ("wo1", 2 * D), ("bqk1", 4)]
    + [(f"{n}{l}", w) for l in range(2) for n, w in
       (("qkv2_", 1536), ("wo2_", 4 * D), ("w1_", 2 * HID), ("w2_", 3 * D), ("b1_", 6), ("ln2_", 2))]
    + [("qkv3", 3 * D), ("wo3", D)]
    + [("f1", 512), ("f2", 512), ("h1", 2048), ("h2", 2048), ("w3", 4 * D), ("s4", 16)])
WEIGHT_CUTS = [0, WEIGHTS["qkv2_0"][0], WEIGHTS["qkv2_1"][0], WEIGHTS["f1"][0], WEIGHTS_WIDTH]
ROWS, ROWS_WIDTH = offsets(
    [("bvg1", 512), ("bo1", D), ("b2_0", D), ("b2_1", D), ("bo3", D), ("s3", D),
     ("g3", 256), ("b3", 256), ("qs0", 256), ("qs1", 256)])
CONSTS, CONSTS_WIDTH = offsets(
    [("ident", 128), ("rot1", 4 * S), ("headmask", H1), ("statemask", H1 * (V1 + 1)), ("chunkdecay", 1),
     ("causal1", 128), ("band_first", 128), ("band", 128),
     ("rot2", NT * 4 * D2),
     ("mask_ij", 128), ("mask_ji", 128), ("shift", 128), ("carry", 128)])


CONST_CUT = CONSTS["band_first"][0]


def build(nc, x, wts, rows, consts, out):
    with ExitStack() as ctx:
        def sb(name, shape, dt=F32):
            return ctx.enter_context(nc.sbuf_tensor(name, shape, dt))

        def sem(name):
            return ctx.enter_context(nc.semaphore(name))

        W = sb("weights", [P, WEIGHTS_WIDTH])
        R = sb("rowconsts", [P, ROWS_WIDTH])
        C = sb("consts_sb", [P, CONSTS_WIDTH])
        xM = sb("x_tokens", [P, G, D])
        xi = sb("x_inner", [P, G, D])
        hT = sb("x_features", [P, 2, S + 1])
        table2 = sb("rotary2", [P, 2, 2, NT, 2, D2])
        mask_ij = sb("mask_ij_bf", [P, P], BF16)
        mask_ji = sb("mask_ji_bf", [P, P], BF16)
        band_bf = sb("band_bf", [P, 2, P], BF16)
        ident_bf = sb("ident_bf", [P, P], BF16)
        neghalf = sb("neghalf", [P, 1])
        stats = sb("bn", [P, 12])
        meanvar = sb("meanvar", [P, 4, 2])
        vareps = sb("vareps", [P, 4])
        rstd = sb("rstd", [P, 4])
        qS = sb("q_strips", [P, 2, S], F32R)
        qS2 = sb("q_strips_shifted", [P, 2, S], F32R)
        kx = sb("k_strips", [P, 2, 4, S], F32R)
        hi3 = sb("hi3", [P, 2, 256], F32R)
        neg3 = sb("negmax3", [P, 16], F32R)
        ARENA = 20100
        arena = sb("arena", [P, ARENA])

        def carve(sizes):
            offs, end = offsets(sizes)
            assert end <= ARENA, end
            return {k: arena[:, a:a + w] for k, (a, w) in offs.items()}

        def w_(name):
            a, n = WEIGHTS[name]
            return W[:, a:a + n]

        def r_(name):
            a, n = ROWS[name]
            return R[:, a:a + n]

        def c_(name):
            a, n = CONSTS[name]
            return C[:, a:a + n]

        ident = c_("ident")
        VW = H1 * (V1 + 1)
        a1 = carve([("qT", 2 * S), ("kT", 2 * S), ("scaled", 4 * S), ("v", G * VW), ("gate", G * 256),
                    ("kM", 2 * S), ("state", 2 * VW), ("statetmp", VW), ("on", 256), ("cen", 512), ("sq", 256),
                    ("cg", 512), ("y", 512), ("yT", 512), ("z", 256), ("den", 16), ("mu", 16), ("gvar", 32),
                    ("grstd", 32), ("qx", 2048), ("PT", 2 * 2048)])
        qT1 = a1["qT"].rearrange("p (b s) -> p b s", b=2)
        kT1 = a1["kT"].rearrange("p (b s) -> p b s", b=2)
        scaled1 = a1["scaled"].rearrange("p (k s) -> p k s", k=4)
        v1 = a1["v"].rearrange("p (g h d) -> p g h d", g=G, h=H1)
        gate1 = a1["gate"].rearrange("p (g d) -> p g d", g=G)
        kM1 = a1["kM"].rearrange("p (g d) -> p g d", g=G)
        state = a1["state"].rearrange("p (b d) -> p b d", b=2)
        cen1 = a1["cen"].rearrange("p (i h d) -> p i h d", i=2, h=H1)
        on1 = a1["on"].rearrange("p (h d) -> p h d", h=H1)
        sq1 = a1["sq"].rearrange("p (h d) -> p h d", h=H1)
        cg1 = a1["cg"].rearrange("p (i h d) -> p i h d", i=2, h=H1)
        y1 = a1["y"].rearrange("p (i d) -> p i d", i=2)
        yT1 = a1["yT"].rearrange("p (i d) -> p i d", i=2)
        z1 = a1["z"].rearrange("p (i d) -> p i d", i=2)
        gvar1 = a1["gvar"].rearrange("p (i d) -> p i d", i=2)
        grstd1 = a1["grstd"].rearrange("p (i d) -> p i d", i=2)
        qx1 = [a1[n].rearrange("p (h d) -> p h d", h=H1) for n in ("qx", "scaled")]
        PT1 = a1["PT"].rearrange("p (i h d) -> p i h d", i=2, h=H1)

        VA = H2 * (D2 + 1)
        a2 = carve([("kz", 2 * H2 * 192), ("sq", 1024), ("qk", 4096), ("qT", 2 * S), ("sm", 2 * 1024),
                    ("PT", 2 * 1024), ("vA", 4 * VA), ("vS", 4 * VA), ("o", 1024), ("oT", 1024), ("hn", 256),
                    ("ss", 32), ("rn", 32), ("mx", 8), ("rs", 8)])
        kz = a2["kz"].rearrange("p (i h j) -> p i h j", i=2, h=H2)
        sq2 = a2["sq"]
        qk2 = a2["qk"][:, 0:2048].rearrange("p (i d) -> p i d", i=2)
        straight2 = a2["qk"][:, 2048:3072]
        swapped2 = a2["qk"][:, 3072:4096]
        gel2 = a2["qk"][:, 0:1024].rearrange("p (i d) -> p i d", i=2)
        hh2 = a2["qk"][:, 1024:4096].rearrange("p (b k s) -> p b k s", b=2, k=3)
        qT2 = a2["qT"].rearrange("p (i m d) -> p i m d", i=2, m=4)
        sm2 = a2["sm"].rearrange("p (i h j) -> p i h j", i=2, h=H2)
        PT2 = a2["PT"].rearrange("p (i h j) -> p i h j", i=2, h=H2)
        vA2 = a2["vA"].rearrange("p (i h d) -> p i h d", i=4, h=H2)
        vS2 = a2["vS"].rearrange("p (i h d) -> p i h d", i=4, h=H2)
        o2 = a2["o"].rearrange("p (i h d) -> p i h d", i=2, h=H2)
        oT2 = a2["oT"].rearrange("p (i m d) -> p i m d", i=2, m=4)
        hn2 = a2["hn"].rearrange("p (i d) -> p i d", i=2)
        ss2 = a2["ss"].rearrange("p (i d) -> p i d", i=2)
        rn2 = a2["rn"].rearrange("p (i d) -> p i d", i=2)

        NSLOT = 8
        a3 = carve([("QS", G * S), ("PT", NSLOT * S), ("KS", G * S), ("vp", G * S), ("oS", 512), ("oN", G * D),
                    ("cen", 1024), ("n", 256), ("sq", 256), ("z", 256), ("mu", 32), ("rs", 128),
                    ("mx", 32), ("r", 16)])
        PT3 = a3["PT"].rearrange("p (i d) -> p i d", i=NSLOT)
        QS = a3["QS"].rearrange("p (g h r) -> p g h r", g=G, h=H3)
        KS = a3["KS"].rearrange("p (g h r) -> p g h r", g=G, h=H3)
        vp = a3["vp"].rearrange("p (g h r) -> p g h r", g=G, h=H3)
        oS3 = a3["oS"]
        oN3 = a3["oN"].rearrange("p (g h d) -> p g h d", g=G, h=H3)
        cen3 = a3["cen"].rearrange("p (i h d) -> p i h d", i=NT, h=32)
        n3 = a3["n"].rearrange("p (h d) -> p h d", h=32)
        sq3 = a3["sq"].rearrange("p (h d) -> p h d", h=32)
        z3 = a3["z"].rearrange("p (i d) -> p i d", i=2)
        rs3 = a3["rs"].rearrange("p (i d) -> p i d", i=NT)
        var3 = a3["z"][:, 0:128].rearrange("p (i d) -> p i d", i=NT)
        mx3 = a3["mx"].rearrange("p (i t h) -> p i t h", i=2, t=NT)
        r3 = a3["r"].rearrange("p (t h) -> p t h", t=NT)

        a4 = carve([("h0", 2 * 4 * S), ("h1", 2 * 4 * S), ("silu", 1024), ("z", 256), ("t", 256)])
        h04 = a4["h0"].rearrange("p (b k s) -> p b k s", b=2, k=4)
        h14 = a4["h1"].rearrange("p (b k s) -> p b k s", b=2, k=4)
        silu4 = a4["silu"].rearrange("p (i s) -> p i s", i=2)
        z4 = a4["z"].rearrange("p (i d) -> p i d", i=2)
        t4 = a4["t"].rearrange("p (i d) -> p i d", i=2)

        psum = [ctx.enter_context(nc.psum_tensor(f"bank{i}", [P, 512], F32)) for i in range(8)]

        loaded = [sem(f"weights_loaded{i}") for i in range(4)]
        rows_loaded = sem("rows_loaded")
        consts_loaded = [sem(f"consts_loaded{i}") for i in range(2)]
        zeros_ready = sem("zeros_ready")
        kx_blank = sem("kx_blank")
        arrived = sem("arrived")
        go = sem("go")
        settle = sem("settle")
        cleared = []

        def counter(name):
            s = sem(name)
            cleared.append(s)
            return s

        retention_done = counter("retention_done")
        x_loaded = [counter(f"x_loaded{b}") for b in range(2)]
        stored = counter("stored")
        tables_ready = counter("tables_ready")
        dve_step = counter("dve_step")
        pool_step = counter("pool_step")
        pe_xT, xT_ready = counter("pe_xT"), counter("xT_ready")
        var_ready, rstd_ready = counter("var_ready"), counter("rstd_ready")
        xM_ready = counter("xM_ready")
        (pe_qk1, qk1_scaled, qkT_ready, pe_vg, gate_pre, gate_ready, pe_kM, kM_ready, ones_ready, xb1_ready,
         qx_ready, pe_sc, PT1_ready, pe_o1, pe_kv, state_ready, on_ready, cen_ready, gvar_ready, grstd_ready,
         cg_ready, y_ready, pe_yT, yT_ready, pe_wo1, z1_ready) = (counter(n) for n in (
             "pe_qk1", "qk1_scaled", "qkT_ready", "pe_vg", "gate_pre", "gate_ready", "pe_kM", "kM_ready",
             "ones_ready", "xb1_ready", "qx_ready", "pe_sc", "PT1_ready", "pe_o1", "pe_kv", "state_ready",
             "on_ready", "cen_ready", "gvar_ready", "grstd_ready", "cg_ready", "y_ready", "pe_yT", "yT_ready",
             "pe_wo1", "z1_ready"))
        (pads_ready, pe_hT, hT_ready, pe_q, pe_k, pe_v, sq_ready, ss_ready, rn_ready, qn_ready, swapped_ready,
         rot_ready, pe_qT, pe_kT, qT_ready, kz_ready, vA_ready, pe_S, smx_ready, P_ready, pe_PT,
         PT2_ready, pe_O, o_ready, pe_oT, oT_ready, pe_wo2, xa_ready, pe_hs, hs_kept, hn_ready, pe_wg, pe_wa, gel_ready,
         hh_ready, xb2_ready, pe_w2, xf_ready) = (counter(n) for n in (
             "pads_ready", "pe_hT", "hT_ready", "pe_q", "pe_k", "pe_v", "sq_ready", "ss_ready", "rn_ready",
             "qn_ready", "swapped_ready", "rot_ready", "pe_qT", "pe_kT", "qT_ready", "kz_ready", "vA_ready",
             "pe_S", "smx_ready", "P_ready", "pe_PT", "PT2_ready", "pe_O", "o_ready", "pe_oT",
             "oT_ready", "pe_wo2", "xa_ready", "pe_hs", "hs_kept", "hn_ready", "pe_wg", "pe_wa", "gel_ready", "hh_ready",
             "xb2_ready", "pe_w2", "xf_ready"))
        vS_landed = [counter(f"vS_landed{i}") for i in range(4)]
        (strips_blank, pe_qkv3, cen3_ready, v3_ready, strips_ready, pe_qS, pe_kS, qS_ready,
         kxa_ready, kxd_ready, pe_A, mx_ready, negmax_ready, pe_qS2, qS2_ready, pe_B, E_ready, pe_V, oS_ready,
         pe_oS, oN_ready, pe_oN, oNT_ready, pe_wo3, z3_ready) = (counter(n) for n in (
             "strips_blank", "pe_qkv3", "cen3_ready", "v3_ready", "strips_ready",
             "pe_qS", "pe_kS", "qS_ready", "kxa_ready", "kxd_ready", "pe_A", "mx_ready", "negmax_ready",
             "pe_qS2", "qS2_ready", "pe_B", "E_ready", "pe_V", "oS_ready", "pe_oS", "oN_ready", "pe_oN",
             "oNT_ready", "pe_wo3", "z3_ready"))
        xb3_ready = counter("xb3_ready")
        hi_ready, hi_placed = counter("hi_ready"), counter("hi_placed")
        (pe_f1, pe_f2, silu_ready, h0_ready, pe_h1, h1_ready, pe_h2, h2_ready, pe_w3, z4_scaled, out_ready) = (
            counter(n) for n in ("pe_f1", "pe_f2", "silu_ready", "h0_ready", "pe_h1", "h1_ready", "pe_h2",
                                 "h2_ready", "pe_w3", "z4_scaled", "out_ready"))

        place = {}
        last = [None] * 8
        turn = [0]

        def take(pe, key, until, bank=None):
            if bank is None:
                bank = turn[0] % 7
                turn[0] += 1
            for s, v in last[bank] or []:
                pe.wait_ge(s, v)
            last[bank] = until
            place[key] = bank
            return psum[bank]

        def held(key):
            return psum[place[key]]

        def hn_seen(n):
            l, g = divmod(n, G)
            return (2 + G) * l + 2 + g + 1

        def retention_end(eng):
            eng.drain().then_inc(retention_done, 1)
            eng.wait_ge(retention_done, 4)

        def pair_end(eng, it):
            eng.drain().then_inc(arrived, 1)
            eng.wait_ge(go, it + 1)
            eng.sem_inc(settle)

        PASS_A = [(t, h, n, (t + 1) * P) for t, n in ((0, 4), (1, 2), (2, 1), (3, 1)) for h in range(0, 4, n)]
        PASS_B = [(t, h, n, (NT - t) * P) for t, n in ((0, 1), (1, 1), (2, 2), (3, 4)) for h in range(0, 4, n)]
        NA, NB = len(PASS_A), len(PASS_B)

        vS_count, total = {}, [0] * 4
        for n in range(2 * G):
            total[n % 4] += 16
            vS_count[n] = total[n % 4]
            if n % NT < NT - 1:
                total[(n + 1) % 4] += 16

        FIRST_TILES = (0,)

        LN1, LN2, LN3, LN4 = 0, 8, 32, 40

        def tile(t):
            return slice(1 + t * P, 1 + (t + 1) * P)

        block = ctx.enter_context(nc.Block())

        @block.tensor
        def _(pe):
            def transposes(bank, sources, n=None):
                for i, src in enumerate(sources):
                    mm = pe.transpose(bank[:, i * P:(i + 1) * P], src, ident)
                return mm

            def features(c, b, ready, count):
                bank = take(pe, ("xT", c), [(xT_ready, c + 1)])
                pe.wait_ge(ready, count)
                transposes(bank, [xM[:, 4 * b + t, :] for t in range(NT)]).then_inc(pe_xT, 1)

            def retention():
                for b in range(2):
                    features(b, b, x_loaded[b], 16)
                for b in range(2):
                    pe.wait_ge(xT_ready, b + 1)
                    for kind in range(4):
                        i = 4 * b + kind
                        bank = take(pe, ("qk1", i), [(qk1_scaled, i + 1)])
                        pe.matmul(bank[:], w_("qk1")[:, kind * P:(kind + 1) * P], hT[:, b, 1:S + 1],
                                  start=True, stop=True).then_inc(pe_qk1, 1)
                    for t in range(NT):
                        g = 4 * b + t
                        bank = take(pe, ("vg", g), [(gate_pre, g + 1)])
                        pe.matmul(bank[:], hT[:, b, tile(t)], w_("vg1"), start=True, stop=True).then_inc(pe_vg, 1)
                for b in range(2):
                    pe.wait_ge(qkT_ready, 2 * b + 2)
                    bank = take(pe, ("kM", b), [(kM_ready, b + 1)])
                    transposes(bank, [kT1[:, b, t * P:(t + 1) * P] for t in range(NT)]).then_inc(pe_kM, 1)

                def scores(g):
                    b, t = divmod(g, NT)
                    for c in range(4):
                        pe.wait_ge(qx_ready, 4 * g + c + 1)
                        bank = take(pe, ("sc", g, c), [(PT1_ready, 4 * g + c + 1)])
                        pe.matmul(bank[:], kT1[:, b, t * P:(t + 1) * P], qx1[g % 2][:, 4 * c:4 * c + 4, :],
                                  start=True, stop=True).then_inc(pe_sc, 1)

                def outputs(g):
                    b, t = divmod(g, NT)
                    bank = take(pe, ("o1", g), [(on_ready, g + 1)], bank=7)
                    if g == 0:
                        pe.wait_ge(ones_ready, 1)
                    if t:
                        pe.wait_ge(state_ready, 3 * b + t)
                        pe.matmul(bank[:, 0:VW], qT1[:, b, t * P:(t + 1) * P], state[:, b, :],
                                  start=True, stop=False, skip_group_check=True)
                    for h in range(H1):
                        if h % 4 == 0:
                            pe.wait_ge(PT1_ready, 4 * g + h // 4 + 1)
                        mm = pe.matmul(bank[:, 17 * h:17 * h + 17], PT1[:, g % 2, h, :], v1[:, g, h, :],
                                       start=(t == 0 and h == 0), stop=(h == H1 - 1), skip_group_check=True)
                    mm.then_inc(pe_o1, 1)
                    if t < NT - 1:
                        bank = take(pe, ("kv", g), [(state_ready, 3 * b + t + 1)])
                        if t == 0:
                            pe.wait_ge(kM_ready, b + 1)
                        pe.matmul(bank[:, 0:VW], kM1[:, g, :], v1[:, g, :, :].rearrange("p h d -> p (h d)"),
                                  start=True, stop=True).then_inc(pe_kv, 1)

                def project(g):
                    pe.wait_ge(y_ready, g + 1)
                    bank = take(pe, ("yT", g), [(yT_ready, g + 1)])
                    transposes(bank, [y1[:, g % 2, 0:P], y1[:, g % 2, P:2 * P]]).then_inc(pe_yT, 1)
                    bank = take(pe, ("wo1", g), [(z1_ready, g + 1)])
                    pe.wait_ge(yT_ready, g + 1)
                    for k in range(2):
                        mm = pe.matmul(bank[:, 0:P], yT1[:, g % 2, k * P:(k + 1) * P],
                                       w_("wo1")[:, k * P:(k + 1) * P], start=(k == 0), stop=(k == 1))
                    mm.then_inc(pe_wo1, 1)

                for s in range(G + 3):
                    if s < G:
                        scores(s)
                    if 1 <= s <= G:
                        outputs(s - 1)
                    if s >= 3:
                        project(s - 3)

            def window_layer(l):
                src = xM if l == 0 else xi
                for s in range(G + 5):
                    g = s
                    if g < G:
                        n = G * l + g
                        b, t = divmod(g, NT)
                        if t == 0:
                            i = 4 * l + b
                            bank = take(pe, ("hT", i), [(hT_ready, i + 1)])
                            if l == 0:
                                pe.wait_ge(xM_ready, NT * (b + 1))
                            else:
                                pe.wait_ge(xf_ready, NT * (b + 1))
                            transposes(bank, [src[:, 4 * b + j, :] for j in range(NT)]).then_inc(pe_hT, 1)
                            pe.wait_ge(hT_ready, i + 1)
                        for j, (name, done, until) in enumerate((("q", pe_q, (swapped_ready, 2 * n + 1)),
                                                                 ("k", pe_k, (swapped_ready, 2 * n + 2)),
                                                                 ("v", pe_v, (vA_ready, n + 1)))):
                            bank = take(pe, (name, n), [until])
                            pe.matmul(bank[:], hT[:, b, t * P:(t + 1) * P], w_(f"qkv2_{l}")[:, 512 * j:512 * j + 512],
                                      start=True, stop=True).then_inc(done, 1)
                    g = s - 4
                    if 0 <= g < G:
                        n = G * l + g
                        pe.wait_ge(xa_ready, n + 1)
                        bank = take(pe, ("hs", n), [(hs_kept, n + 1)])
                        mm = pe.matmul(bank[:, 0:64], c_("shift"), xi[:, g, 64:P], start=True, stop=(g % NT == 0))
                        if g % NT:
                            mm = pe.matmul(bank[:, 0:64], c_("carry"), xi[:, g - 1, 64:P], start=False, stop=True)
                        mm.then_inc(pe_hs, 1)
                    g = s - 1
                    if 0 <= g < G:
                        n = G * l + g
                        pe.wait_ge(qn_ready, n + 1)
                        bank = take(pe, ("qT", n), [(qT_ready, n + 1)])
                        transposes(bank, [qk2[:, g % 2, i * P:(i + 1) * P] for i in range(4)]).then_inc(pe_qT, 1)
                        bank = take(pe, ("kT", n), [(kz_ready, n + 1)])
                        transposes(bank, [qk2[:, g % 2, 512 + i * P:512 + (i + 1) * P] for i in range(4)])\
                            .then_inc(pe_kT, 1)
                    g = s - 2
                    if 0 <= g < G:
                        n = G * l + g
                        pe.wait_ge(P_ready, n + 1)
                        for c in range(2):
                            bank = take(pe, ("PT", n, c), [(PT2_ready, 2 * n + c + 1)])
                            transposes(bank, [sm2[:, g % 2, 4 * c + i, :] for i in range(4)]).then_inc(pe_PT, 1)
                    g = s - 1
                    if 0 <= g < G:
                        n = G * l + g
                        pe.wait_ge(qT_ready, n + 1)
                        pe.wait_ge(kz_ready, n + 1)
                        for c in range(2):
                            bank = take(pe, ("S", n, c), [(smx_ready, 2 * n + c + 1)])
                            first = 0 if g % NT == 0 else 1
                            pe.matmul(bank[:].rearrange("p (h j) -> p h j", h=4), ident_bf[:],
                                      band_bf[:, first:first + 1, :].to_broadcast([P, 4, P]),
                                      start=True, stop=False, skip_group_check=True)
                            for i in range(4):
                                h = 4 * c + i
                                for w in range(2):
                                    mm = pe.matmul(bank[64 * w:64 * w + 64, i * P:(i + 1) * P],
                                                   qT2[:, g % 2, h // 2, 64 * w:64 * w + 64],
                                                   kz[:, g % 2, h, 64 * w:64 * w + P],
                                                   start=False, stop=True, skip_group_check=True)
                            mm.then_inc(pe_S, 1)
                    g = s - 3
                    if 0 <= g < G:
                        n = G * l + g
                        pe.wait_ge(o_ready, 2 * n + 2)
                        bank = take(pe, ("oT", n), [(oT_ready, n + 1)])
                        transposes(bank, [o2[:, g % 2, 2 * i:2 * i + 2, :].rearrange("p h d -> p (h d)")
                                          for i in range(4)]).then_inc(pe_oT, 1)
                    g = s - 2
                    if 0 <= g < G:
                        n = G * l + g
                        pe.wait_ge(vA_ready, n + 1)
                        pe.wait_ge(vS_landed[n % 4], vS_count[n])
                        for c in range(2):
                            pe.wait_ge(PT2_ready, 2 * n + c + 1)
                            bank = take(pe, ("O", n, c), [(o_ready, 2 * n + c + 1)])
                            for i in range(4):
                                h = 4 * c + i
                                for w, v in ((0, vS2), (1, vA2)):
                                    mm = pe.matmul(bank[64 * w:64 * w + 64, 65 * i:65 * i + 65],
                                                   PT2[:, g % 2, h, 64 * w:64 * w + 64], v[:, n % 4, h, :],
                                                   start=True, stop=True)
                            mm.then_inc(pe_O, 1)
                    g = s - 3
                    if 0 <= g < G:
                        n = G * l + g
                        bank = take(pe, ("wo2", n), [(xa_ready, n + 1)])
                        pe.wait_ge(oT_ready, n + 1)
                        for k in range(4):
                            mm = pe.matmul(bank[:, 0:P], oT2[:, g % 2, k, :],
                                           w_(f"wo2_{l}")[:, k * P:(k + 1) * P], start=(k == 0), stop=(k == 3))
                        mm.then_inc(pe_wo2, 1)
                    if s >= 5:
                        normed(l, s - 5)
                    if s >= G + 2:
                        widen(l, 0, s - G - 2)

            def gelu_layer(l):
                for kb in range(3):
                    widen(l, 1, kb)
                for g in range(G):
                    n = G * l + g
                    b, t = divmod(g, NT)
                    if t == 0:
                        pe.wait_ge(hh_ready, 3 * (2 * l + b) + 3)
                    bank = take(pe, ("w2", n), [(xf_ready, n + 1)])
                    for kb, K in enumerate(KB):
                        mm = pe.matmul(bank[:, 0:P], hh2[0:K, b, kb, t * P:(t + 1) * P],
                                       w_(f"w2_{l}")[0:K, kb * P:(kb + 1) * P], start=(kb == 0), stop=(kb == 2))
                    mm.then_inc(pe_w2, 1)

            def widen(l, b, kb):
                i, K = 3 * (2 * l + b) + kb, KB[kb]
                pe.wait_ge(hT_ready, 4 * l + 2 + b + 1)
                for name, at, done, until in (("wg", HID, pe_wg, gel_ready), ("wa", 0, pe_wa, hh_ready)):
                    bank = take(pe, (name, i), [(until, i + 1)])
                    pe.matmul(bank[0:K, :], w_(f"w1_{l}")[:, at + kb * P:at + kb * P + K],
                              hT[:, b, 1:S + 1], start=True, stop=True).then_inc(done, 1)

            def normed(l, g):
                n = G * l + g
                b, t = divmod(g, NT)
                i = 4 * l + 2 + b
                if t == 0:
                    take(pe, ("hT", i), [(hT_ready, i + 1)], bank=7)
                pe.wait_ge(hn_ready, n + 1)
                mm = pe.transpose(held(("hT", i))[:, t * P:(t + 1) * P], hn2[:, g % 2, :], ident)
                mm.then_inc(pe_hT, 1)

            def causal():
                def project(b):
                    features(2 + b, b, xM_ready, G + NT * (b + 1))
                    pe.wait_ge(xT_ready, 2 + b + 1)
                    for t in range(NT):
                        g = NT * b + t
                        bank = take(pe, ("qkv3", g), [(v3_ready, g + 1)])
                        pe.matmul(bank[:, 0:384], hT[:, b, tile(t)], w_("qkv3"), start=True, stop=True)\
                            .then_inc(pe_qkv3, 1)

                def strips(u):
                    b, quad = divmod(u, 4)
                    pe.wait_ge(strips_ready, NT * (b + 1))
                    pe.wait_ge(hi_placed, NT * (b + 1))
                    for name, src, done, until in (
                            ("qS", QS, pe_qS, [(qS_ready, u + 1)]),
                            ("kS", KS, pe_kS, [(kxa_ready, u + 1), (kxd_ready, u + 1)])):
                        bank = take(pe, (name, u), until)
                        transposes(bank, [src[:, 4 * b + t, 4 * quad:4 * quad + 4, :].rearrange("p h r -> p (h r)")
                                          for t in range(NT)]).then_inc(done, 1)

                def pass_a(u, j):
                    t, h, n, wide = PASS_A[j]
                    i = NA * u + j
                    bank = take(pe, ("A", i), [(mx_ready, i + 1)])
                    view = bank[:, 0:n * wide].rearrange("p (h j) -> p h j", h=n)
                    pe.matmul(view, qS[:, u % 2, t * P:(t + 1) * P], kx[:, u % 2, h:h + n, 0:wide],
                              start=True, stop=False, skip_group_check=True)
                    pe.matmul(view[:, :, wide - P:wide], ident_bf[:],
                              mask_ij[:].unsqueeze(1).to_broadcast([P, n, P]),
                              start=False, stop=True, skip_group_check=True).then_inc(pe_A, 1)

                def strips_shifted(u):
                    b, quad = divmod(u, 4)
                    pe.wait_ge(negmax_ready, u + 1)
                    bank = take(pe, ("qS2", u), [(qS2_ready, u + 1)])
                    transposes(bank, [QS[:, 4 * b + t, 4 * quad:4 * quad + 4, :].rearrange("p h r -> p (h r)")
                                      for t in range(NT)]).then_inc(pe_qS2, 1)

                def pass_b(u, j):
                    t, h, n, wide = PASS_B[j]
                    i = NB * u + j
                    bank = take(pe, ("B", i), [(E_ready, i + 1)])
                    for k in range(n):
                        pe.matmul(bank[:, k * wide:(k + 1) * wide], kx[:, u % 2, h + k, t * P:(t + 1) * P],
                                  qS2[:, u % 2, t * P:S], start=(k == 0), stop=False, skip_group_check=True)
                    view = bank[:, 0:n * wide].rearrange("p (h j) -> p h j", h=n)
                    pe.matmul(view[:, :, 0:P], ident_bf[:], mask_ji[:].unsqueeze(1).to_broadcast([P, n, P]),
                              start=False, stop=True, skip_group_check=True).then_inc(pe_B, 1)

                def values(u, j):
                    b, quad = divmod(u, 4)
                    t, h, n, wide = PASS_B[j]
                    i = NB * u + j
                    if j == 0:
                        take(pe, ("o3", u), [(oS_ready, u + 1)], bank=7)
                        pe.wait_ge(v3_ready, NT * (b + 1))
                    pe.wait_ge(E_ready, i + 1)
                    for k in range(n):
                        mm = pe.matmul(psum[7][32 * (h + k):32 * (h + k) + 32, t * P:S],
                                       vp[:, 4 * b + t, 4 * quad + h + k, :],
                                       PT3[:, i % NSLOT, k * wide:(k + 1) * wide],
                                       start=(t == 0), stop=(t == NT - 1), skip_group_check=True)
                    mm.then_inc(pe_V, 1)

                def head_outputs(u):
                    bank = take(pe, ("oS", u), [(oN_ready, u + 1)])
                    pe.wait_ge(oS_ready, u + 1)
                    transposes(bank, [oS3[:, t * P:(t + 1) * P] for t in range(NT)]).then_inc(pe_oS, 1)

                def gather(b):
                    pe.wait_ge(oN_ready, 4 * (b + 1))
                    bank = take(pe, ("oN", b), [(oNT_ready, b + 1)])
                    transposes(bank, [oN3[:, 4 * b + t, :, :].rearrange("p h d -> p (h d)") for t in range(NT)])\
                        .then_inc(pe_oN, 1)

                def finish(g):
                    b, t = divmod(g, NT)
                    pe.wait_ge(oNT_ready, b + 1)
                    bank = take(pe, ("wo3", g), [(z3_ready, g + 1)])
                    pe.matmul(bank[:, 0:P], hT[:, b, tile(t)], w_("wo3"), start=True, stop=True).then_inc(pe_wo3, 1)

                LAG = 3
                project(0)
                strips(0)
                for s in range(G + 1):
                    if s < G:
                        pe.wait_ge(qS_ready, s + 1)
                        pe.wait_ge(kxa_ready, s + 1)
                        pe.wait_ge(kxd_ready, s + 1)
                    if s == 0:
                        for j in range(NA):
                            pass_a(s, j)
                        project(1)
                    else:
                        strips_shifted(s - 1)
                        if s < G:
                            pass_a(s, 0)
                        pe.wait_ge(qS2_ready, s)
                        for j in range(NB):
                            pass_b(s - 1, j)
                            if s < G and j + 1 < NA:
                                pass_a(s, j + 1)
                            if j >= LAG:
                                values(s - 1, j - LAG)
                    if s + 1 < G:
                        strips(s + 1)
                    if s >= 1:
                        for j in range(NB - LAG, NB):
                            values(s - 1, j)
                        head_outputs(s - 1)
                    if s == 5:
                        gather(0)
                    if s in (6, 7):
                        finish(2 * s - 12)
                        finish(2 * s - 11)
                gather(1)
                for g in range(NT, G):
                    finish(g)
            def mlp():
                for b in range(2):
                    features(4 + b, b, xM_ready, 2 * G + NT * (b + 1))
                for b in range(2):
                    pe.wait_ge(xT_ready, 4 + b + 1)
                    for k in range(4):
                        i = 4 * b + k
                        for name, done, until in (("f1", pe_f1, silu_ready), ("f2", pe_f2, h0_ready)):
                            bank = take(pe, (name, i), [(until, i + 1)])
                            pe.matmul(bank[:], w_(name)[:, k * P:(k + 1) * P], hT[:, b, 1:S + 1],
                                      start=True, stop=True).then_inc(done, 1)
                def hidden(name, src, have, done, until, b):
                    pe.wait_ge(have, 4 * (b + 1))
                    for k in range(4):
                        i = 4 * b + k
                        bank = take(pe, (name, i), [(until, i + 1)])
                        for c in range(4):
                            mm = pe.matmul(bank[:], w_(name)[:, 512 * c + k * P:512 * c + (k + 1) * P],
                                           src[:, b, c, :], start=(c == 0), stop=(c == 3))
                        mm.then_inc(done, 1)

                def narrow(b):
                    pe.wait_ge(h2_ready, 4 * (b + 1))
                    for t in range(NT):
                        g = NT * b + t
                        bank = take(pe, ("w3", g), [(z4_scaled, g + 1)])
                        for c in range(4):
                            mm = pe.matmul(bank[:, 0:P], h04[:, b, c, t * P:(t + 1) * P],
                                           w_("w3")[:, c * P:(c + 1) * P], start=(c == 0), stop=(c == 3))
                        mm.then_inc(pe_w3, 1)

                for b in range(2):
                    hidden("h1", h04, h0_ready, pe_h1, h1_ready, b)
                for b in range(2):
                    hidden("h2", h14, h1_ready, pe_h2, h2_ready, b)
                    if b == 1:
                        narrow(0)
                narrow(1)

            pe.wait_ge(consts_loaded[0], 16)
            pe.wait_ge(loaded[0], 16)
            with pe.Fori(0, 2) as it:
                retention()
                retention_end(pe)
                pe.wait_ge(consts_loaded[1], 16)
                pe.wait_ge(tables_ready, 1)
                for l in range(2):
                    pe.wait_ge(loaded[1 + l], 16)
                    if l == 0:
                        pe.wait_ge(pads_ready, 1)
                    window_layer(l)
                    gelu_layer(l)
                pe.wait_ge(strips_blank, 2)
                pe.wait_ge(kx_blank, 1)
                causal()
                pe.wait_ge(loaded[3], 16)
                mlp()
                pair_end(pe, it)

        @block.vector
        def _(dve):
            steps = [0]

            def link(ins):
                steps[0] += 1
                ins.then_inc(dve_step, 1)
                dve.wait_ge(dve_step, steps[0])

            def norm_stats(k, parts):
                for i, part in enumerate(parts):
                    link(dve.bn_stats(stats[:, 6 * i:6 * i + 6], part))
                link(dve.bn_aggr(meanvar[:, k % 4, :], stats[:, 0:6 * len(parts)]))
                dve.tensor_scalar(vareps[:, k % 4:k % 4 + 1], meanvar[:, k % 4, 1:2], EPS, None, ALU.add)\
                    .then_inc(var_ready, 1)

            def norm_apply(k, dst, src):
                dve.wait_ge(rstd_ready, k + 1)
                return dve.tensor_scalar(dst, src, meanvar[:, k % 4, 0:1], rstd[:, k % 4:k % 4 + 1],
                                         ALU.subtract, ALU.mult)

            def retention():
                dve.memset(v1[:, :, :, V1:V1 + 1], 1.0).then_inc(ones_ready, 1)
                dve.wait_ge(rows_loaded, 16)
                for b in range(2):
                    for kind in range(4):
                        i = 4 * b + kind
                        if b:
                            dve.wait_ge(qkT_ready, kind // 2 + 1)
                        dve.wait_ge(pe_qk1, i + 1)
                        dve.scalar_tensor_tensor(out=scaled1[:, kind, :], in0=held(("qk1", i))[:],
                                                 scalar=w_("bqk1")[:, kind:kind + 1],
                                                 in1=c_("rot1")[:, kind * S:(kind + 1) * S],
                                                 op0=ALU.add, op1=ALU.mult).then_inc(qk1_scaled, 1)
                    for t in range(NT):
                        g = 4 * b + t
                        dve.wait_ge(pe_vg, g + 1)
                        dve.tensor_tensor(v1[:, g, :, 0:V1],
                                          held(("vg", g))[:, 0:256].rearrange("p (h d) -> p h d", h=H1),
                                          r_("bvg1")[:, 0:256].rearrange("p (h d) -> p h d", h=H1), ALU.add)
                        dve.tensor_tensor(gate1[:, g, :], held(("vg", g))[:, 256:512], r_("bvg1")[:, 256:512],
                                          ALU.add).then_inc(gate_pre, 1)

                def masked(g):
                    if g >= 2:
                        dve.wait_ge(pe_o1, g - 1)
                    for c in range(4):
                        dve.wait_ge(pe_sc, 4 * g + c + 1)
                        dve.tensor_tensor(PT1[:, g % 2, 4 * c:4 * c + 4, :],
                                          held(("sc", g, c))[:].rearrange("p (h j) -> p h j", h=4),
                                          c_("causal1").unsqueeze(1).to_broadcast([P, 4, P]), ALU.mult)\
                            .then_inc(PT1_ready, 1)

                def update_state(g):
                    b, t = divmod(g, NT)
                    dve.wait_ge(pe_kv, 3 * b + t + 1)
                    tmp = a1["statetmp"]
                    if t == 0:
                        dve.tensor_tensor(state[:, b, :], held(("kv", g))[:, 0:VW], c_("statemask"), ALU.mult)\
                            .then_inc(state_ready, 1)
                    else:
                        link(dve.tensor_tensor(tmp, held(("kv", g))[:, 0:VW], c_("statemask"), ALU.mult))
                        dve.scalar_tensor_tensor(out=state[:, b, :], in0=state[:, b, :], scalar=c_("chunkdecay"),
                                                 in1=tmp, op0=ALU.mult, op1=ALU.add).then_inc(state_ready, 1)

                def normalise(g):
                    o = held(("o1", g))[:, 0:VW].rearrange("p (h d) -> p h d", h=H1)
                    total = o[:, :, V1:V1 + 1]
                    den, mu = a1["den"].unsqueeze(2), a1["mu"].unsqueeze(2)
                    dve.wait_ge(pe_o1, g + 1)
                    if g:
                        dve.wait_ge(gvar_ready, g)
                    link(dve.tensor_scalar(mu, total, -1.0, None, ALU.mult))
                    link(dve.tensor_tensor(den, total, mu, ALU.max))
                    link(dve.tensor_scalar(den, den, 1.0, None, ALU.max))
                    link(dve.reciprocal(den, den))
                    dve.tensor_tensor(on1[:], o[:, :, 0:V1], den.to_broadcast([P, H1, V1]), ALU.mult)\
                        .then_inc(on_ready, 1)
                    dve.wait_ge(on_ready, g + 1)
                    link(dve.tensor_reduce(a1["mu"], on1[:], AX, ALU.add))
                    link(dve.tensor_scalar(mu, mu, 1.0 / V1, None, ALU.mult))
                    if g >= 2:
                        dve.wait_ge(cg_ready, g - 1)
                    dve.tensor_tensor(cen1[:, g % 2], on1[:], mu.to_broadcast([P, H1, V1]), ALU.subtract)\
                        .then_inc(cen_ready, 1)
                    dve.wait_ge(cen_ready, g + 1)
                    link(dve.tensor_tensor(sq1[:], cen1[:, g % 2], cen1[:, g % 2], ALU.mult))
                    link(dve.tensor_reduce(a1["mu"], sq1[:], AX, ALU.add))
                    dve.tensor_scalar(gvar1[:, g % 2, :], a1["mu"], 1.0 / V1, EPS, ALU.mult, ALU.add)\
                        .then_inc(gvar_ready, 1)

                def gated(g):
                    dve.wait_ge(grstd_ready, g + 1)
                    dve.wait_ge(cg_ready, g + 1)
                    if g >= 2:
                        dve.wait_ge(pe_yT, g - 1)
                    dve.tensor_tensor(y1[:, g % 2, :].rearrange("p (h d) -> p h d", h=H1), cg1[:, g % 2],
                                      grstd1[:, g % 2, :].unsqueeze(2).to_broadcast([P, H1, V1]), ALU.mult)\
                        .then_inc(y_ready, 1)

                def residual(g):
                    dve.wait_ge(pe_wo1, g + 1)
                    dve.wait_ge(xb1_ready, 1)
                    if g >= 2:
                        dve.wait_ge(xM_ready, g - 1)
                    dve.tensor_tensor(z1[:, g % 2, :], held(("wo1", g))[:, 0:P], xi[:, g, :], ALU.add)\
                        .then_inc(z1_ready, 1)
                    dve.wait_ge(z1_ready, g + 1)
                    norm_stats(LN1 + g, [z1[:, g % 2, :]])

                tables()
                for s in range(G + 5):
                    if s < G:
                        masked(s)
                    if 2 <= s <= G + 1:
                        gated(s - 2)
                    if 4 <= s:
                        if s - 4 < G:
                            residual(s - 4)
                        if s >= 5:
                            norm_apply(LN1 + s - 5, xM[:, s - 5, :], z1[:, (s - 5) % 2, :]).then_inc(xM_ready, 1)
                    if 1 <= s <= G:
                        if (s - 1) % NT < NT - 1:
                            update_state(s - 1)
                        normalise(s - 1)

            def tables():
                dve.wait_ge(consts_loaded[1], 16)
                for dst, name in ((band_bf[:, 0, :], "band_first"), (band_bf[:, 1, :], "band"),
                                  (mask_ij[:], "mask_ij"), (mask_ji[:], "mask_ji"), (ident_bf[:], "ident")):
                    dve.tensor_copy(dst, c_(name))
                rot2 = c_("rot2").rearrange("p (k t d) -> p k t d", k=4, t=NT)
                for l in range(2):
                    gains = r_(f"qs{l}").rearrange("p (k d) -> p k d", k=4)
                    for k in range(4):
                        ins = dve.tensor_tensor(table2[:, l, k % 2, :, k // 2, :], rot2[:, k, :, :],
                                                gains[:, k:k + 1, :].to_broadcast([P, NT, D2]), ALU.mult)
                ins.then_inc(tables_ready, 1)

            def gated_hidden(l, b, kb):
                i, K = 3 * (2 * l + b) + kb, KB[kb]
                dve.wait_ge(gel_ready, i + 1)
                dve.wait_ge(pe_wa, i + 1)
                dve.scalar_tensor_tensor(out=hh2[0:K, b, kb, :], in0=held(("wa", i))[0:K, :],
                                         scalar=w_(f"b1_{l}")[0:K, kb:kb + 1], in1=gel2[0:K, i % 2, :],
                                         op0=ALU.add, op1=ALU.mult).then_inc(hh_ready, 1)

            def window_layer(l):
                src = xM if l == 0 else xi
                if l == 0:
                    dve.wait_ge(tables_ready, 1)
                first = LN2 + G * l

                def shifted_stats(g):
                    n = G * l + g
                    dve.wait_ge(pe_hs, n + 1)
                    if n >= 2:
                        dve.wait_ge(pe_hT, hn_seen(n - 2))
                    dve.tensor_copy(hn2[:, g % 2, 64:P], held(("hs", n))[:, 0:64]).then_inc(hs_kept, 1)
                    dve.wait_ge(hs_kept, n + 1)
                    dve.wait_ge(xa_ready, n + 1)
                    norm_stats(first + g, [xi[:, g, 0:64], hn2[:, g % 2, 64:P]])

                def shifted_normed(g):
                    norm_apply(first + g, hn2[:, g % 2, 0:64], xi[:, g, 0:64])
                    norm_apply(first + g, hn2[:, g % 2, 64:P], hn2[:, g % 2, 64:P]).then_inc(hn_ready, 1)

                for s in range(G + 5):
                    g = s
                    if g < G:
                        n = G * l + g
                        t = g % NT
                        dve.wait_ge(sq_ready, 2 * n + 2)
                        link(dve.tensor_reduce(ss2[:, g % 2, :], sq2.rearrange("p (h d) -> p h d", d=D2),
                                               AX, ALU.add))
                        dve.tensor_scalar(ss2[:, g % 2, :], ss2[:, g % 2, :], 1e-24, None, ALU.max)\
                            .then_inc(ss_ready, 1)
                        if n:
                            dve.wait_ge(qn_ready, n)
                        for i, name in enumerate("qk"):
                            raw = held((name, n))[:].rearrange("p (h d) -> p h d", h=H2)
                            plain = straight2[:, 512 * i:512 * i + 512].rearrange("p (h d) -> p h d", h=H2)
                            swap = swapped2[:, 512 * i:512 * i + 512].rearrange("p (h d) -> p h d", h=H2)
                            dve.tensor_tensor(plain, raw, table2[:, l, 0, t, i:i + 1, :].to_broadcast([P, H2, D2]),
                                              ALU.mult)
                            dve.tensor_tensor(swap[:, :, 0:32], raw[:, :, 32:64],
                                              table2[:, l, 1, t, i:i + 1, 0:32].to_broadcast([P, H2, 32]), ALU.mult)
                            dve.tensor_tensor(swap[:, :, 32:64], raw[:, :, 0:32],
                                              table2[:, l, 1, t, i:i + 1, 32:64].to_broadcast([P, H2, 32]),
                                              ALU.mult).then_inc(swapped_ready, 1)
                        if g in FIRST_TILES:
                            dve.wait_ge(swapped_ready, 2 * n + 2)
                            dve.tensor_tensor(straight2, straight2, swapped2, ALU.add).then_inc(rot_ready, 1)
                    if s >= 5:
                        shifted_normed(s - 5)
                    if 4 <= s < G + 4:
                        shifted_stats(s - 4)
                    g = s - 1
                    if 0 <= g < G:
                        n = G * l + g
                        if n >= 2:
                            dve.wait_ge(pe_PT, 2 * (n - 1))
                        for c in range(2):
                            dve.wait_ge(pe_S, 2 * n + c + 1)
                            scores = held(("S", n, c))[:].rearrange("p (h j) -> p h j", h=4)
                            mx = a2["mx"][:, 4 * c:4 * c + 4]
                            link(dve.tensor_reduce(mx, scores, AX, ALU.max))
                            dve.tensor_tensor(sm2[:, g % 2, 4 * c:4 * c + 4, :], scores,
                                              mx.unsqueeze(2).to_broadcast([P, 4, P]), ALU.subtract)\
                                .then_inc(smx_ready, 1)
                    g = s
                    if g < G:
                        n = G * l + g
                        if n >= 2:
                            dve.wait_ge(pe_kT, n - 1)
                        dve.wait_ge(rn_ready, n + 1)
                        dve.wait_ge(rot_ready, n + 1)
                        dve.tensor_tensor(qk2[:, g % 2, :].rearrange("p (h d) -> p h d", d=D2),
                                          straight2.rearrange("p (h d) -> p h d", d=D2),
                                          rn2[:, g % 2, :].unsqueeze(2).to_broadcast([P, 2 * H2, D2]), ALU.mult)\
                            .then_inc(qn_ready, 1)
                    g = s - 2
                    if 0 <= g < G:
                        n = G * l + g
                        if n >= 2:
                            dve.wait_ge(pe_oT, n - 1)
                        for c in range(2):
                            dve.wait_ge(pe_O, 2 * n + c + 1)
                            o = held(("O", n, c))[:, 0:260].rearrange("p (h d) -> p h d", h=4)
                            rs = a2["rs"][:, 4 * c:4 * c + 4].unsqueeze(2)
                            link(dve.reciprocal(rs, o[:, :, D2:D2 + 1]))
                            dve.tensor_tensor(o2[:, g % 2, 4 * c:4 * c + 4, :], o[:, :, 0:D2],
                                              rs.to_broadcast([P, 4, D2]), ALU.mult).then_inc(o_ready, 1)
                    g = s - 3
                    if 0 <= g < G:
                        n = G * l + g
                        dve.wait_ge(pe_wo2, n + 1)
                        dve.tensor_tensor(xi[:, g, :], held(("wo2", n))[:, 0:P], src[:, g, :], ALU.add)\
                            .then_inc(xa_ready, 1)
                    if s >= G + 3:
                        gated_hidden(l, 0, s - G - 3)

            def gelu_layer(l):
                gated_hidden(l, 0, 2)
                for kb in range(3):
                    gated_hidden(l, 1, kb)
                last_norm = LN2 + 2 * G
                dve.wait_ge(xb2_ready, l + 1)
                for g in range(G):
                    n = G * l + g
                    dve.wait_ge(pe_w2, n + 1)
                    dve.tensor_tensor(xi[:, g, :], held(("w2", n))[:, 0:P], xi[:, g, :], ALU.add)\
                        .then_inc(xf_ready, 1)
                    if l == 1:
                        dve.wait_ge(xf_ready, n + 1)
                        norm_stats(last_norm + g, [xi[:, g, :]])
                        if g >= 1:
                            norm_apply(last_norm + g - 1, xM[:, g - 1, :], xi[:, g - 1, :]).then_inc(xM_ready, 1)
                if l == 1:
                    norm_apply(last_norm + G - 1, xM[:, G - 1, :], xi[:, G - 1, :]).then_inc(xM_ready, 1)

            def causal():
                def stats3(g):
                    bank = held(("qkv3", g))[:, 0:256].rearrange("p (h d) -> p h d", h=32)
                    dve.wait_ge(pe_qkv3, g + 1)
                    mu = a3["mu"]
                    link(dve.tensor_reduce(mu, bank, AX, ALU.add))
                    link(dve.tensor_scalar(mu, mu, 1.0 / D3, None, ALU.mult))
                    dve.tensor_tensor(cen3[:, g % NT], bank, mu.unsqueeze(2).to_broadcast([P, 32, D3]),
                                      ALU.subtract).then_inc(cen3_ready, 1)
                    dve.wait_ge(cen3_ready, g + 1)
                    link(dve.tensor_tensor(sq3[:], cen3[:, g % NT], cen3[:, g % NT], ALU.mult))
                    link(dve.tensor_reduce(mu, sq3[:], AX, ALU.add))
                    link(dve.tensor_scalar(var3[:, g % NT, :], mu, 1.0 / D3, EPS, ALU.mult, ALU.add))

                def roots():
                    v, y = a3["z"][:, 0:128], a3["rs"]
                    half, t = a3["z"][:, 128:256], a3["n"][:, 0:128]
                    link(dve.tensor_single_scalar(y.bitcast(I32), v.bitcast(I32), 1, ALU.arith_shift_right))
                    link(dve.tensor_scalar(y.bitcast(I32), y.bitcast(I32), -1.0, float(0x5F3759DF),
                                           ALU.mult, ALU.add))
                    link(dve.tensor_scalar(half, v, -0.5, None, ALU.mult))
                    for _ in range(4):
                        link(dve.tensor_tensor(t, y, y, ALU.mult))
                        link(dve.tensor_tensor(t, t, half, ALU.mult))
                        link(dve.scalar_tensor_tensor(out=y, in0=t, scalar=1.5, in1=y, op0=ALU.add, op1=ALU.mult))

                def cut(g):
                    if g:
                        dve.wait_ge(strips_ready, g)
                    link(dve.tensor_tensor(n3[:], cen3[:, g % NT],
                                           rs3[:, g % NT, :].unsqueeze(2).to_broadcast([P, 32, D3]), ALU.mult))
                    flat, scale = a3["n"], float(D) ** -0.25
                    link(dve.scalar_tensor_tensor(out=flat, in0=flat, scalar=scale, in1=r_("g3"),
                                                  op0=ALU.mult, op1=ALU.mult))
                    link(dve.scalar_tensor_tensor(out=flat, in0=r_("b3"), scalar=scale, in1=flat,
                                                  op0=ALU.mult, op1=ALU.add))
                    if g >= 2:
                        dve.wait_ge(hi_placed, g - 1)
                    dve.tensor_copy(hi3[:, g % 2, :], n3[:].rearrange("p h d -> p (h d)")).then_inc(hi_ready, 1)
                    dve.wait_ge(hi_ready, g + 1)
                    hi = hi3[:, g % 2, :].bitcast(F32).rearrange("p (h d) -> p h d", h=32)
                    if g == 0:
                        dve.wait_ge(strips_blank, 2)
                        dve.wait_ge(kx_blank, 1)
                    dve.tensor_tensor(QS[:, g, :, 16:24], n3[:, 0:16, :], hi[:, 0:16, :], ALU.subtract)
                    dve.tensor_tensor(KS[:, g, :, 8:16], n3[:, 16:32, :], hi[:, 16:32, :], ALU.subtract)\
                        .then_inc(strips_ready, 1)

                def kstrips(u):
                    dve.wait_ge(pe_kS, u + 1)
                    if u >= 2:
                        dve.wait_ge(pe_B, NB * (u - 1))
                    for h in (2, 3):
                        ins = dve.tensor_copy(kx[32 * h:32 * h + 32, u % 2, h, :],
                                              held(("kS", u))[32 * h:32 * h + 32, :])
                    ins.then_inc(kxd_ready, 1)

                def maxima(u):
                    b, quad = divmod(u, 4)
                    for j, (t, h, n, wide) in enumerate(PASS_A):
                        i = NA * u + j
                        dve.wait_ge(pe_A, i + 1)
                        dve.tensor_reduce(mx3[:, u % 2, t, h:h + n],
                                          held(("A", i))[:, 0:n * wide].rearrange("p (h j) -> p h j", h=n),
                                          AX, ALU.max).then_inc(mx_ready, 1)
                    dve.wait_ge(mx_ready, NA * (u + 1))
                    mx = mx3[:, u % 2]
                    if u:
                        dve.wait_ge(negmax_ready, u)
                    neg = neg3[:].bitcast(F32).rearrange("p (t h) -> p t h", t=NT)
                    link(dve.tensor_scalar(neg3[:].rearrange("p (t h) -> p t h", t=NT), mx, -1.0, None, ALU.mult))
                    dst = QS[:, 4 * b:4 * b + 4, 4 * quad:4 * quad + 4, :]
                    dve.tensor_copy(dst[:, :, :, 24], neg)
                    dve.scalar_tensor_tensor(out=dst[:, :, :, 25], in0=mx, scalar=-1.0, in1=neg,
                                             op0=ALU.mult, op1=ALU.subtract).then_inc(negmax_ready, 1)

                def weighted(u):
                    b, quad = divmod(u, 4)
                    dve.wait_ge(pe_oS, u + 1)
                    o = held(("oS", u))[:].rearrange("p (t h r) -> p t h r", t=NT, h=4)
                    link(dve.reciprocal(r3[:], o[:, :, :, D3]))
                    dve.tensor_tensor(oN3[:, 4 * b:4 * b + 4, 4 * quad:4 * quad + 4, :], o[:, :, :, 0:D3],
                                      r3[:].unsqueeze(3).to_broadcast([P, NT, 4, D3]), ALU.mult)\
                        .then_inc(oN_ready, 1)

                def finish(g):
                    dve.wait_ge(pe_wo3, g + 1)
                    dve.wait_ge(xb3_ready, 1)
                    if g >= 2:
                        dve.wait_ge(xM_ready, 2 * G + g - 1)
                    dve.tensor_tensor(z3[:, g % 2, :], held(("wo3", g))[:, 0:P], xi[:, g, :], ALU.add)\
                        .then_inc(z3_ready, 1)
                    dve.wait_ge(z3_ready, g + 1)
                    norm_stats(LN3 + g, [z3[:, g % 2, :]])
                    if g >= 1:
                        norm_apply(LN3 + g - 1, xM[:, g - 1, :], z3[:, (g - 1) % 2, :]).then_inc(xM_ready, 1)

                for g in range(NT):
                    stats3(g)
                roots()
                for g in range(NT):
                    cut(g)
                kstrips(0)
                for s in range(G + 1):
                    if s in (7, 8):
                        finish(2 * s - 14)
                        finish(2 * s - 13)
                    if s < G:
                        maxima(s)
                    if s + 1 < G:
                        kstrips(s + 1)
                    if s == 0:
                        for g in range(NT, G):
                            stats3(g)
                        roots()
                    elif s <= 2:
                        cut(2 * s + 2)
                        cut(2 * s + 3)
                    if s >= 1 and s - 1 < G:
                        weighted(s - 1)
                for g in range(NT, G):
                    finish(g)
                norm_apply(LN3 + G - 1, xM[:, G - 1, :], z3[:, (G - 1) % 2, :]).then_inc(xM_ready, 1)

            def mlp():
                for i in range(2 * 4):
                    b, k = divmod(i, 4)
                    dve.wait_ge(silu_ready, i + 1)
                    dve.wait_ge(pe_f2, i + 1)
                    dve.scalar_tensor_tensor(out=h04[:, b, k, :], in0=held(("f2", i))[:],
                                             scalar=w_("s4")[:, 4 + k:5 + k], in1=silu4[:, i % 2, :],
                                             op0=ALU.mult, op1=ALU.mult).then_inc(h0_ready, 1)
                for g in range(G):
                    dve.wait_ge(pe_w3, g + 1)
                    dve.tensor_tensor(t4[:, g % 2, :], held(("w3", g))[:, 0:P], r_("s3"), ALU.mult)\
                        .then_inc(z4_scaled, 1)
                    dve.wait_ge(z4_scaled, g + 1)
                    if g >= 2:
                        dve.wait_ge(out_ready, g - 1)
                    link(dve.tensor_tensor(z4[:, g % 2, :], t4[:, g % 2, :], xM[:, g, :], ALU.add))
                    norm_stats(LN4 + g, [z4[:, g % 2, :]])
                    if g >= 1:
                        norm_apply(LN4 + g - 1, xi[:, g - 1, :], z4[:, (g - 1) % 2, :]).then_inc(out_ready, 1)
                norm_apply(LN4 + G - 1, xi[:, G - 1, :], z4[:, (G - 1) % 2, :]).then_inc(out_ready, 1)

            dve.memset(neghalf[:], -0.5)
            dve.memset(hT[64:P, :, 0:1], 0.0)
            dve.drain().then_inc(zeros_ready, 1)
            dve.wait_ge(consts_loaded[0], 16)
            dve.wait_ge(loaded[0], 16)
            with dve.Fori(0, 2) as it:
                retention()
                retention_end(dve)
                for l in range(2):
                    dve.wait_ge(loaded[1 + l], 16)
                    window_layer(l)
                    gelu_layer(l)
                causal()
                dve.wait_ge(loaded[3], 16)
                mlp()
                pair_end(dve, it)

        @block.scalar
        def _(act):
            def evac(dst, src):
                return act.activation(dst, src, ACT.Copy)

            def features(c, b):
                act.wait_ge(pe_xT, c + 1)
                evac(hT[:, b, 1:S + 1], held(("xT", c))[:]).then_inc(xT_ready, 1)

            def retention():
                for b in range(2):
                    features(b, b)
                for g in range(G):
                    act.wait_ge(gate_pre, g + 1)
                    act.activation(gate1[:, g, :], gate1[:, g, :], ACT.Silu).then_inc(gate_ready, 1)
                for b in range(2):
                    act.wait_ge(pe_kM, b + 1)
                    evac(kM1[:, 4 * b:4 * b + 4, :].rearrange("p g d -> p (g d)"), held(("kM", b))[:])\
                        .then_inc(kM_ready, 1)
                def expand(g):
                    b, t = divmod(g, NT)
                    act.wait_ge(qkT_ready, 4)
                    for h in range(H1):
                        if h % 4 == 0 and g >= 2:
                            act.wait_ge(pe_sc, 4 * (g - 2) + h // 4 + 1)
                        ins = act.activation(qx1[g % 2][:, h, :], qT1[:, b, t * P:(t + 1) * P], ACT.Copy,
                                             scale=c_("headmask")[:, h:h + 1])
                        if h % 4 == 3:
                            ins.then_inc(qx_ready, 1)

                expand(0)
                expand(1)
                for s in range(G + 3):
                    if s >= 3:
                        g = s - 3
                        act.wait_ge(pe_yT, g + 1)
                        if g >= 2:
                            act.wait_ge(pe_wo1, g - 1)
                        evac(yT1[:, g % 2, :], held(("yT", g))[:, 0:256]).then_inc(yT_ready, 1)
                    if s + 2 < G:
                        expand(s + 2)

            def window_layer(l):
                for s in range(G + 3):
                    if s == G + 1:
                        normed_features(l, 0)
                    g = s
                    if g < G:
                        n = G * l + g
                        b, t = divmod(g, NT)
                        if t == 0:
                            i = 4 * l + b
                            act.wait_ge(pe_hT, (2 + G) * l + b + 1)
                            evac(hT[0:64, b, 0:S], held(("hT", i))[0:64, :])
                            evac(hT[64:P, b, 1:S + 1], held(("hT", i))[64:P, :]).then_inc(hT_ready, 1)
                        if n:
                            act.wait_ge(ss_ready, n)
                        for j, (name, done) in enumerate((("q", pe_q), ("k", pe_k))):
                            act.wait_ge(done, n + 1)
                            act.activation(sq2[:, 512 * j:512 * j + 512], held((name, n))[:], ACT.Square)\
                                .then_inc(sq_ready, 1)
                    g = s - 1
                    if 0 <= g < G:
                        n = G * l + g
                        if n >= 2:
                            act.wait_ge(pe_S, 2 * (n - 1))
                        act.wait_ge(pe_qT, n + 1)
                        evac(qT2[:, g % 2].rearrange("p m d -> p (m d)"), held(("qT", n))[:]).then_inc(qT_ready, 1)
                        act.wait_ge(pe_kT, n + 1)
                        src = held(("kT", n))[:].rearrange("p (m d) -> p m d", m=4)
                        if n:
                            act.wait_ge(pe_S, 2 * n)
                        for half in range(2):
                            rows = slice(64 * half, 64 * half + 64)
                            ins = evac(kz[rows, g % 2, half:H2:2, 64:192], src[rows, :, :])
                            if g % NT < NT - 1:
                                ins = evac(kz[rows, (g + 1) % 2, half:H2:2, 0:64], src[rows, :, 64:P])
                        ins.then_inc(kz_ready, 1)
                    g = s - 2
                    if 0 <= g < G:
                        n = G * l + g
                        if n >= 2:
                            act.wait_ge(pe_O, 2 * (n - 1))
                        for c in range(2):
                            act.wait_ge(pe_PT, 2 * n + c + 1)
                            evac(PT2[:, g % 2, 4 * c:4 * c + 4, :].rearrange("p h j -> p (h j)"),
                                 held(("PT", n, c))[:]).then_inc(PT2_ready, 1)
                    g = s
                    if g < G:
                        n = G * l + g
                        act.wait_ge(pe_v, n + 1)
                        if n >= 4:
                            act.wait_ge(pe_O, 2 * (n - 2))
                        evac(vA2[:, n % 4, :, 0:D2], held(("v", n))[:].rearrange("p (h d) -> p h d", h=H2))\
                            .then_inc(vA_ready, 1)
                    g = s - 3
                    if 0 <= g < G:
                        n = G * l + g
                        act.wait_ge(pe_oT, n + 1)
                        if n >= 2:
                            act.wait_ge(pe_wo2, n - 1)
                        evac(oT2[:, g % 2].rearrange("p m d -> p (m d)"), held(("oT", n))[:]).then_inc(oT_ready, 1)
                    g = s - 1
                    if 0 <= g < G:
                        n = G * l + g
                        act.wait_ge(smx_ready, 2 * n + 2)
                        act.activation(sm2[:, g % 2], sm2[:, g % 2], ACT.Exp).then_inc(P_ready, 1)

            def normed_features(l, b):
                i = 4 * l + 2 + b
                act.wait_ge(pe_hT, (2 + G) * l + 2 + NT * (b + 1))
                act.activation(hT[:, b, 1:S + 1], held(("hT", i))[:], ACT.Identity,
                               bias=w_(f"ln2_{l}")[:, 1:2], scale=w_(f"ln2_{l}")[:, 0:1]).then_inc(hT_ready, 1)

            def gelu_layer(l):
                for b in range(2):
                    for kb, K in enumerate(KB):
                        if (b, kb) == (0, 2):
                            normed_features(l, 1)
                        i = 3 * (2 * l + b) + kb
                        act.wait_ge(pe_wg, i + 1)
                        if i >= 2:
                            act.wait_ge(hh_ready, i - 1)
                        act.activation(gel2[0:K, i % 2, :], held(("wg", i))[0:K, :], ACT.Gelu,
                                       bias=w_(f"b1_{l}")[0:K, 3 + kb:4 + kb], scale=1.0).then_inc(gel_ready, 1)

            def causal():
                features(2, 0)
                act.wait_ge(strips_blank, 2)
                act.wait_ge(kx_blank, 1)
                def values(g):
                    act.wait_ge(cen3_ready, g + 1)
                    evac(vp[:, g, :, 0:D3], held(("qkv3", g))[:, 256:384].rearrange("p (h d) -> p h d", h=H3))\
                        .then_inc(v3_ready, 1)

                def place_high(g):
                    act.wait_ge(hi_ready, g + 1)
                    hi = hi3[:, g % 2, :].bitcast(F32).rearrange("p (h d) -> p h d", h=32)
                    evac(QS[:, g, :, 0:8], hi[:, 0:16, :])
                    evac(QS[:, g, :, 8:16], hi[:, 0:16, :])
                    evac(KS[:, g, :, 0:8], hi[:, 16:32, :])
                    evac(KS[:, g, :, 16:24], hi[:, 16:32, :]).then_inc(hi_placed, 1)

                for g in range(NT):
                    values(g)
                for g in range(NT):
                    place_high(g)

                def gather(b):
                    act.wait_ge(pe_oN, b + 1)
                    evac(hT[:, b, 1:S + 1], held(("oN", b))[:]).then_inc(oNT_ready, 1)

                def strips(u):
                    act.wait_ge(pe_qS, u + 1)
                    if u >= 2:
                        act.wait_ge(pe_A, NA * (u - 1))
                    evac(qS[:, u % 2, :], held(("qS", u))[:]).then_inc(qS_ready, 1)
                    act.wait_ge(pe_kS, u + 1)
                    if u >= 2:
                        act.wait_ge(pe_B, NB * (u - 1))
                    for h in (0, 1):
                        ins = evac(kx[32 * h:32 * h + 32, u % 2, h, :], held(("kS", u))[32 * h:32 * h + 32, :])
                    ins.then_inc(kxa_ready, 1)

                strips(0)
                for s in range(G + 1):
                    u = s - 1
                    if u >= 0:
                        act.wait_ge(pe_qS2, u + 1)
                        evac(qS2[:, u % 2, :], held(("qS2", u))[:]).then_inc(qS2_ready, 1)
                        for j, (t, h, n, wide) in enumerate(PASS_B):
                            i = NB * u + j
                            act.wait_ge(pe_B, i + 1)
                            if i >= NSLOT:
                                act.wait_ge(pe_V, i - NSLOT + 1)
                            act.activation(PT3[:, i % NSLOT, 0:n * wide], held(("B", i))[:, 0:n * wide], ACT.Exp)\
                                .then_inc(E_ready, 1)
                    if s == 0:
                        features(3, 1)
                    if s + 1 < G:
                        strips(s + 1)
                    if u >= 0:
                        act.wait_ge(pe_V, NB * (u + 1))
                        if u:
                            act.wait_ge(pe_oS, u)
                        evac(oS3, psum[7][:]).then_inc(oS_ready, 1)
                    if s == 0:
                        for g in range(NT, G):
                            values(g)
                    elif s <= 2:
                        place_high(2 * s + 2)
                        place_high(2 * s + 3)
                    elif s == 5:
                        gather(0)
                gather(1)

            def mlp():
                for b in range(2):
                    features(4 + b, b)
                for i in range(2 * 4):
                    act.wait_ge(pe_f1, i + 1)
                    if i >= 2:
                        act.wait_ge(h0_ready, i - 1)
                    act.activation(silu4[:, i % 2, :], held(("f1", i))[:], ACT.Silu,
                                   scale=w_("s4")[:, i % 4:i % 4 + 1]).then_inc(silu_ready, 1)
                for name, dst, done, ready, at in (("h1", h14, pe_h1, h1_ready, 8), ("h2", h04, pe_h2, h2_ready, 12)):
                    for i in range(2 * 4):
                        b, k = divmod(i, 4)
                        act.wait_ge(done, i + 1)
                        act.activation(dst[:, b, k, :], held((name, i))[:], ACT.Gelu,
                                       scale=w_("s4")[:, at + k:at + k + 1]).then_inc(ready, 1)

            act.dma_start(R[:], rows.to_broadcast([P, ROWS_WIDTH])).then_inc(rows_loaded, 16)
            act.dma_start(C[:, CONST_CUT:], consts[:, CONST_CUT:]).then_inc(consts_loaded[1], 16)
            for i in range(1, 4):
                act.dma_start(W[:, WEIGHT_CUTS[i]:WEIGHT_CUTS[i + 1]], wts[:, WEIGHT_CUTS[i]:WEIGHT_CUTS[i + 1]])\
                    .then_inc(loaded[i], 16)
            act.wait_ge(zeros_ready, 1)
            with act.Fori(0, 2) as it:
                retention()
                retention_end(act)
                act.wait_ge(pads_ready, 1)
                for l in range(2):
                    act.wait_ge(loaded[1 + l], 16)
                    window_layer(l)
                    gelu_layer(l)
                causal()
                act.wait_ge(loaded[3], 16)
                mlp()
                pair_end(act, it)

        @block.gpsimd
        def _(pool):
            def root(k):
                pool.wait_ge(var_ready, k + 1)
                pool.tensor_tensor(rstd[:, k % 4:k % 4 + 1], vareps[:, k % 4:k % 4 + 1], neghalf[:], ALU.pow)\
                    .then_inc(rstd_ready, 1)

            def retention():
                for b in range(2):
                    pool.wait_ge(x_loaded[b], 16)
                pool.tensor_tensor(xi[:], xM[:], r_("bo1").unsqueeze(1).to_broadcast([P, G, D]), ALU.add)\
                    .then_inc(xb1_ready, 1)
                for b in range(2):
                    for side, dst in ((0, qT1), (1, kT1)):
                        pool.wait_ge(qk1_scaled, 4 * b + 2 * side + 2)
                        pool.tensor_tensor(dst[:, b, :], scaled1[:, 2 * side, :], scaled1[:, 2 * side + 1, :],
                                           ALU.add).then_inc(qkT_ready, 1)
                for s in range(G + 4):
                    g = s
                    if g < G:
                        pool.wait_ge(cen_ready, g + 1)
                        pool.wait_ge(gate_ready, g + 1)
                        if g >= 2:
                            pool.wait_ge(y_ready, g - 1)
                        pool.tensor_tensor(cg1[:, g % 2], cen1[:, g % 2],
                                           gate1[:, g, :].rearrange("p (h d) -> p h d", h=H1), ALU.mult)\
                            .then_inc(cg_ready, 1)
                        pool.wait_ge(gvar_ready, g + 1)
                        pool.tensor_tensor(grstd1[:, g % 2, :], gvar1[:, g % 2, :],
                                           neghalf[:].to_broadcast([P, H1]), ALU.pow).then_inc(grstd_ready, 1)
                    if s >= 3 and s - 3 < G:
                        root(LN1 + s - 3)

            def window_layer(l):
                for s in range(G + 4):
                    g = s
                    if g < G:
                        n = G * l + g
                        pool.wait_ge(ss_ready, n + 1)
                        pool.tensor_tensor(rn2[:, g % 2, :], ss2[:, g % 2, :], neghalf[:].to_broadcast([P, 16]),
                                           ALU.pow).then_inc(rn_ready, 1)
                        if g not in FIRST_TILES:
                            pool.wait_ge(swapped_ready, 2 * n + 2)
                            if n:
                                pool.wait_ge(rot_ready, n)
                            pool.tensor_tensor(straight2, straight2, swapped2, ALU.add).then_inc(rot_ready, 1)
                    if s >= 4:
                        root(LN2 + G * l + s - 4)

            def gelu_layer(l):
                pool.wait_ge(pe_hs, G * (l + 1))
                pool.wait_ge(hn_ready, G * (l + 1))
                ins = pool.tensor_tensor(xi[:], xi[:], r_(f"b2_{l}").unsqueeze(1).to_broadcast([P, G, D]), ALU.add)
                if l == 0:
                    ins.then_inc(xb2_ready, 1)
                else:
                    ins.then_inc(pool_step, 1)
                    pool.wait_ge(pool_step, 1)
                    pool.tensor_tensor(xi[:], xi[:], xM[:], ALU.add).then_inc(xb2_ready, 1)
                    pool.memset(QS[:, :, :, 24:32], 0.0)
                    pool.memset(KS[:, :, :, 24:26], 1.0)
                    pool.memset(KS[:, :, :, 26:32], 0.0)
                    pool.memset(vp[:, :, :, D3:D3 + 1], 1.0)
                    pool.memset(vp[:, :, :, D3 + 1:32], 0.0)
                    pool.drain().then_inc(strips_blank, 2)
                    for g in range(G):
                        root(LN2 + 2 * G + g)

            def causal():
                pool.wait_ge(xM_ready, 2 * G)
                pool.tensor_tensor(xi[:], xM[:], r_("bo3").unsqueeze(1).to_broadcast([P, G, D]), ALU.add)\
                    .then_inc(xb3_ready, 1)
                for g in range(G):
                    root(LN3 + g)

            pool.memset(kx[:].bitcast(F32), 0.0).then_inc(kx_blank, 1)
            pool.wait_ge(zeros_ready, 1)
            pool.wait_ge(rows_loaded, 16)
            with pool.Fori(0, 2) as it:
                retention()
                retention_end(pool)
                pool.memset(kz[:], 0.0)
                pool.memset(vS2[:], 0.0)
                pool.drain().then_inc(settle, 1)
                pool.memset(vS2[:, :, :, D2:D2 + 1], 1.0)
                pool.memset(vA2[:, :, :, D2:D2 + 1], 1.0)
                pool.drain().then_inc(pads_ready, 1)
                for l in range(2):
                    window_layer(l)
                    gelu_layer(l)
                causal()
                for g in range(G):
                    root(LN4 + g)
                pair_end(pool, it)

        @block.sync
        def _(sp):
            sp.dma_start(C[:, 0:CONST_CUT], consts[:, 0:CONST_CUT]).then_inc(consts_loaded[0], 16)
            sp.dma_start(W[:, 0:WEIGHT_CUTS[1]], wts[:, 0:WEIGHT_CUTS[1]]).then_inc(loaded[0], 16)
            with sp.Fori(0, 2) as it:
                for b in range(2):
                    sp.dma_start(xM[:, 4 * b:4 * b + 4, :], x[2 * it + b].rearrange("(t p) d -> p t d", p=P))\
                        .then_inc(x_loaded[b], 16)
                sp.wait_ge(pads_ready, 1)
                for l in range(2):
                    for g in range(G):
                        n = G * l + g
                        sp.wait_ge(vA_ready, n + 1)
                        if n >= 4:
                            sp.wait_ge(pe_O, 2 * (n - 3))
                        sp.dma_start(vS2[64:P, n % 4, :, :], vA2[0:64, n % 4, :, :]).then_inc(vS_landed[n % 4], 16)
                        if g % NT < NT - 1:
                            if n >= 3:
                                sp.wait_ge(pe_O, 2 * (n - 2))
                            sp.dma_start(vS2[0:64, (n + 1) % 4, :, :], vA2[64:P, n % 4, :, :])\
                                .then_inc(vS_landed[(n + 1) % 4], 16)
                for g in range(G):
                    b, t = divmod(g, NT)
                    sp.wait_ge(out_ready, g + 1)
                    sp.dma_start(out[2 * it + b].rearrange("(t p) d -> p t d", p=P)[:, t, :], xi[:, g, :])\
                        .then_inc(stored, 16)
                sp.wait_ge(stored, 16 * G)
                sp.wait_ge(arrived, 4 * (it + 1))
                sp.sem_inc(settle)
                for s in cleared:
                    sp.sem_clear(s)
                sp.drain().then_inc(go, 1)


def _layout(inp):
    import numpy as np
    f = {k: np.asarray(v) for k, v in inp.items()}

    def swap(a):
        return a.reshape(a.shape[:-1] + (-1, 2))[..., ::-1].reshape(a.shape)

    def blocks(a):
        return a.reshape(-1, P, a.shape[-1]).transpose(1, 0, 2).reshape(P, -1)

    def padded(a):
        n = -(-a.shape[0] // P) * P
        return np.concatenate([a, np.zeros((n - a.shape[0],) + a.shape[1:], a.dtype)])

    def cols(*vs):
        return np.stack(vs, axis=1)

    w = {"qk1": np.concatenate([f["L0_attn_Wq"], swap(f["L0_attn_Wq"]), f["L0_attn_Wk"], swap(f["L0_attn_Wk"])], 1),
         "vg1": np.concatenate([f["L0_attn_Wv"], f["L0_attn_Wg"]], 1),
         "wo1": blocks(f["L0_attn_Wo"]),
         "bqk1": cols(f["L0_attn_bq"], swap(f["L0_attn_bq"]), f["L0_attn_bk"], swap(f["L0_attn_bk"])),
         "qkv3": np.concatenate([f["L1_attn_Wq"].T, f["L1_attn_Wk"].T, f["L1_attn_Wv"].T], 1),
         "wo3": f["L1_attn_Wo"].T,
         "f1": f["L1_ffn_w1_w"].T, "f2": f["L1_ffn_w2_w"].T, "h1": blocks(f["L1_ffn_h1_w"].T),
         "h2": blocks(f["L1_ffn_h2_w"].T), "w3": blocks(f["L1_ffn_w3_w"].T),
         "s4": np.concatenate([f[n].reshape(4, P).T for n in ("L1_ffn_w1_s", "L1_ffn_w2_s", "L1_ffn_h1_s",
                                                              "L1_ffn_h2_s")], 1)}
    for l in range(2):
        w[f"qkv2_{l}"] = f["L0_ffn_wqkv"][l]
        w[f"wo2_{l}"] = blocks(f["L0_ffn_wo"][l])
        w[f"w1_{l}"] = f["L0_ffn_w1"][l]
        w[f"w2_{l}"] = blocks(padded(f["L0_ffn_w2"][l]))
        b1 = f["L0_ffn_b1"][l]
        w[f"b1_{l}"] = np.concatenate([padded(b1[:HID]).reshape(3, P).T, padded(b1[HID:]).reshape(3, P).T], 1)
        w[f"ln2_{l}"] = cols(f["L0_ffn_ln_g"][l], f["L0_ffn_ln_b"][l])
    wts = np.ascontiguousarray(np.concatenate([w[n] for n in WEIGHTS], 1))

    def halves(a):
        return np.concatenate([a[32:], a[:32]])

    r = {"bvg1": np.concatenate([f["L0_attn_bv"], f["L0_attn_bg"]]), "bo1": f["L0_attn_bo"],
         "b2_0": f["L0_ffn_b2"][0], "b2_1": f["L0_ffn_b2"][1], "bo3": f["L1_attn_bo"], "s3": f["L1_ffn_w3_s"],
         "g3": np.concatenate([np.tile(f["L1_attn_qln_g"], H3), np.tile(f["L1_attn_kln_g"], H3)]),
         "b3": np.concatenate([np.tile(f["L1_attn_qln_b"], H3), np.tile(f["L1_attn_kln_b"], H3)])}
    for l in range(2):
        q, k = f["L0_ffn_q_scale"][l], f["L0_ffn_k_scale"][l]
        r[f"qs{l}"] = np.concatenate([q, halves(q), k, halves(k)])
    rows = np.ascontiguousarray(np.concatenate([r[n] for n in ROWS])[None, :])

    i = np.arange(P)
    pos = np.arange(S)
    f32 = np.float32
    c = {"ident": np.eye(P)}
    angle = np.repeat((1.0 / 10000.0 ** np.linspace(0.0, 1.0, K1 // 2, dtype=f32)).astype(f32), 2)
    turn = (pos[:, None].astype(f32) * angle[None, :]).astype(f32).astype(np.float64)
    gamma = 1.0 - 2.0 ** (-5.0 - np.arange(H1))
    dist = np.cumsum(gamma[:, None] ** pos[None, :], axis=1)
    local = pos % P
    qdecay = gamma[:, None] ** local[None, :] / np.sqrt(dist)
    kdecay = gamma[:, None] ** (-local[None, :]) * K1 ** -0.5
    sign = np.where(np.arange(K1) % 2 == 0, -1.0, 1.0)
    straight, swapped = np.cos(turn).T, (np.sin(turn) * sign).T
    c["rot1"] = np.concatenate([(d[:, None, :] * m[None, :, :]).reshape(D, S)
                                for d, m in ((qdecay, straight), (qdecay, swapped),
                                             (kdecay, straight), (kdecay, swapped))], 1)
    head = i // K1
    c["headmask"] = head[:, None] == np.arange(H1)[None, :]
    chunk = gamma[head] ** P
    c["statemask"] = np.repeat(c["headmask"], V1 + 1, axis=1) * chunk[:, None]
    c["chunkdecay"] = chunk[:, None]
    c["causal1"] = i[:, None] <= i[None, :]
    half = np.arange(0, D2, 2, dtype=f32)
    inv = (1.0 / 10000.0 ** (half / f32(D2))).astype(f32)
    fr = (pos[:, None].astype(f32) * inv[None, :]).astype(f32).astype(np.float64)
    fr = np.concatenate([fr, fr], 1)
    base = (half + 0.4 * D2) / (1.4 * D2)
    scale = base[None, :].astype(np.float64) ** ((pos - S // 2) / float(WIN // 2))[:, None]
    scale = np.concatenate([scale, scale], 1)
    sgn = np.where(np.arange(D2) < D2 // 2, -1.0, 1.0)
    tabs = [np.cos(fr) * scale * 8.0, np.sin(fr) * sgn * scale * 8.0, np.cos(fr) / scale, np.sin(fr) * sgn / scale]
    c["rot2"] = np.stack([t.reshape(NT, P, D2).transpose(1, 0, 2) for t in tabs], 1)
    q_, k_ = i[:, None] % WIN, i[None, :]
    allowed = (k_ >= q_) & (k_ <= q_ + WIN)
    c["band"] = np.where(allowed, 0.0, -1e30)
    c["band_first"] = np.where(allowed & ((i[:, None] >= WIN) | (k_ >= WIN)), 0.0, -1e30)
    c["mask_ij"] = np.where(i[None, :] > i[:, None], -1e30, 0.0)
    c["mask_ji"] = c["mask_ij"].T
    c["shift"] = i[None, :] == i[:, None] + 1
    c["carry"] = (i[:, None] == P - 1) & (i[None, :] == 0)
    consts = np.ascontiguousarray(np.concatenate([c[n].reshape(P, -1) for n in CONSTS], 1).astype(f32))
    return {"x": np.ascontiguousarray(f["L0_attn_x"]), "wts": wts, "rows": rows, "consts": consts}


def kernel(**inputs):
    import concourse.bacc as bacc
    from concourse.bass_utils import run_bass_kernel_spmd

    arrays = _layout(inputs)
    nc = bacc.Bacc("TRN2", target_bir_lowering=False, num_devices=1)
    args = [nc.dram_tensor(f"{n}_dram", a.shape, F32, kind="ExternalInput").ap() for n, a in arrays.items()]
    out = nc.dram_tensor("out_dram", arrays["x"].shape, F32, kind="ExternalOutput").ap()
    build(nc, *args, out)
    r = run_bass_kernel_spmd(nc, [{f"{n}_dram": a for n, a in arrays.items()}], core_ids=[0])
    return r.results[0]["out_dram"]
```
